# Optimizing a Trainium2 kernel written in Bass

```python
import numpy as np
import jax
import jax.numpy as jnp

def _softmax(x, axis=-1):
    return jax.nn.softmax(x, axis=axis)

def _gelu(x):
    return jax.nn.gelu(x, approximate=True)

def _silu(x):
    return jax.nn.silu(x)

def _sigmoid(x):
    return jax.nn.sigmoid(x)

def _layernorm(x, axis=-1, eps=1e-05):
    m = jnp.mean(x, axis=axis, keepdims=True)
    v = jnp.var(x, axis=axis, keepdims=True)
    return (x - m) / jnp.sqrt(v + eps)

def _scatter_add(tgt, idx, src, axis=0):
    return tgt.at[idx].add(src)

def _segment_sum(src, seg, n):
    return jax.ops.segment_sum(src, seg, n)
kernel_name = 'mk_gnn_resnorm_d1_gnn_r8_558954'

def setup_inputs(seed: int=0):
    np.random.seed(seed)
    _w = jnp.asarray

    def _rec_inputs():
        import jax
        import jax.numpy as jnp
        _gk = jax.random.key(seed)
        x = -0.0005121 + 1.001 * jax.random.normal(jax.random.fold_in(_gk, 1), (12500, 64), jnp.float32)
        src = jax.random.randint(jax.random.fold_in(_gk, 2), (200000,), 0, 12500, jnp.int32)
        dst = jnp.minimum((12500 * jax.random.uniform(jax.random.fold_in(_gk, 3), (200000,)) ** 2.0).astype(jnp.int32), 99999)
        _o = jnp.argsort(dst, stable=True)
        src = src[_o]
        dst = dst[_o]
        edge_type_64 = jax.random.randint(jax.random.fold_in(_gk, 12), (200000,), 0, 64, jnp.int32)
        edge_weight1 = jax.random.uniform(jax.random.fold_in(_gk, 13), (200000, 1), jnp.float32, 0.0, 0.999998)
        return (x, src, dst, edge_type_64, edge_weight1)
    x, src, dst, edge_type_64, edge_weight1 = _rec_inputs()

    def _L0_gnn_setup():
        import jax, jax.numpy as jnp
        import numpy as np
        N_NODES = 6250
        N_EDGES = 200000
        IN_F = 64
        OUT_F = 64
        NUM_RELS = 64
        NUM_BASES = 64
        BN_EPS = 1e-05
        key = jax.random.key(seed)
        ks = jax.random.split(key, 12)
        node_feats = jax.random.normal(ks[0], (N_NODES, IN_F), dtype=jnp.float32)
        src = jax.random.randint(ks[1], (N_EDGES,), 0, N_NODES, dtype=jnp.int32)
        dst = jax.random.randint(ks[2], (N_EDGES,), 0, N_NODES, dtype=jnp.int32)
        etype = jax.random.randint(ks[3], (N_EDGES,), 0, NUM_RELS, dtype=jnp.int32)
        norm = jax.random.uniform(ks[4], (N_EDGES, 1), dtype=jnp.float32)
        basis = jax.random.normal(ks[5], (NUM_BASES, IN_F, OUT_F), dtype=jnp.float32) * (1.0 / np.sqrt(IN_F))
        comp = jax.random.normal(ks[6], (NUM_RELS, NUM_BASES), dtype=jnp.float32) * (1.0 / np.sqrt(NUM_BASES))
        bias = jnp.zeros((OUT_F,), dtype=jnp.float32)
        res_w = jax.random.normal(ks[7], (OUT_F, IN_F), dtype=jnp.float32) * (1.0 / np.sqrt(IN_F))
        res_b = jnp.zeros((OUT_F,), dtype=jnp.float32)
        gamma = jnp.ones((OUT_F,), dtype=jnp.float32)
        beta = jnp.zeros((OUT_F,), dtype=jnp.float32)
        return {'node_feats': node_feats, 'src': src, 'dst': dst, 'etype': etype, 'norm': norm, 'basis': basis, 'comp': comp, 'bias': bias, 'res_w': res_w, 'res_b': res_b, 'gamma': gamma, 'beta': beta}
    _L0_gnn_all = _L0_gnn_setup()
    _L0_gnn_in = {k: v for k, v in _L0_gnn_all.items() if k in ('basis', 'comp', 'bias', 'res_w', 'res_b', 'gamma', 'beta')}
    del _L0_gnn_all
    return {'x': x, 'src': src, 'dst': dst, 'edge_type_64': edge_type_64, 'edge_weight1': edge_weight1, 'L0_gnn_basis': _L0_gnn_in['basis'], 'L0_gnn_comp': _L0_gnn_in['comp'], 'L0_gnn_bias': _L0_gnn_in['bias'], 'L0_gnn_res_w': _L0_gnn_in['res_w'], 'L0_gnn_res_b': _L0_gnn_in['res_b'], 'L0_gnn_gamma': _L0_gnn_in['gamma'], 'L0_gnn_beta': _L0_gnn_in['beta']}

def reference(x, src, dst, edge_type_64, edge_weight1, L0_gnn_basis, L0_gnn_comp, L0_gnn_bias, L0_gnn_res_w, L0_gnn_res_b, L0_gnn_gamma, L0_gnn_beta):
    import jax
    import jax.numpy as jnp

    def _L0_gnn_ref(node_feats, src, dst, etype, norm, basis, comp, bias, res_w, res_b, gamma, beta):
        import jax, jax.numpy as jnp
        import numpy as np
        N_NODES = 6250
        N_EDGES = 200000
        IN_F = 64
        OUT_F = 64
        NUM_RELS = 64
        NUM_BASES = 64
        BN_EPS = 1e-05
        N = node_feats.shape[0]
        R = comp.shape[0]
        W = jnp.einsum('rb,bio->rio', comp, basis)
        msg = node_feats[src] * norm
        seg = etype.astype(jnp.int32) * N + dst
        s = jax.ops.segment_sum(msg, seg, num_segments=R * N)
        s = s.reshape(R, N, -1)
        h = jnp.einsum('rni,rio->no', s, W) + bias
        h = jax.nn.relu(h)
        res = jax.nn.relu(node_feats @ res_w.T + res_b)
        y = h + res
        mean = jnp.mean(y, axis=0)
        var = jnp.var(y, axis=0)
        return (y - mean) * jax.lax.rsqrt(var + BN_EPS) * gamma + beta
    x = _layernorm(x + _L0_gnn_ref(x, src, dst, edge_type_64, edge_weight1, L0_gnn_basis, L0_gnn_comp, L0_gnn_bias, L0_gnn_res_w, L0_gnn_res_b, L0_gnn_gamma, L0_gnn_beta), axis=-1)
    return x

_drawn_inputs = setup_inputs


def setup_inputs(seed=0):
    import zlib

    import numpy as np

    out = dict(_drawn_inputs(seed))
    spreads = {'L0_gnn_bias': (0.0, 0.359),
     'L0_gnn_res_b': (0.0, 0.331),
     'L0_gnn_gamma': (1.0, 0.2),
     'L0_gnn_beta': (0.0, 0.1)}
    factors = {}
    for name, (base, spread) in spreads.items():
        noise = np.random.default_rng([zlib.crc32(name.encode()), seed]).standard_normal(out[name].shape)
        drawn = base * np.exp(spread * noise) if base else spread * noise
        out[name] = jnp.asarray(drawn.astype(out[name].dtype))
    for name, factor in factors.items():
        out[name] = (out[name] * factor).astype(out[name].dtype)
    return out
```

```python
import concourse.bass as bass
from concourse import mybir
from contextlib import ExitStack

P = 128
N_NODES = 12500
N_EDGES = 200000
F = 64
RELS = 64
BASES = 64
BN_EPS = 1e-05
LN_EPS = 1e-05

NODE_TILES = -(-N_NODES // P)
NODES_PADDED = NODE_TILES * P
ROW = RELS * F
UNIT = 1024
UNITS = ROW // UNIT
BANK = 512

GROUP = 4
EDGE_TILES = -(-N_EDGES // P)
LAST_TILE_ROWS = N_EDGES - (EDGE_TILES - 1) * P
GROUPS = -(-EDGE_TILES // GROUP)
QUADS = 4
SLOTS = GROUP * QUADS
TURNS = GROUPS // QUADS
TILE_COLUMNS = (TURNS + 1) * SLOTS

WINDOW = 128
WIDE = 512
WIDE_WINDOWS = -(-N_NODES // WIDE)
H_COLUMNS = max(WIDE_WINDOWS * WIDE, N_NODES + WINDOW)

GP = 78
GJ = (GROUPS - 1) // GP
GE = GROUP * P
LAST_EDGES = N_EDGES - (GROUPS - 1) * GE

BN_STEPS = 10
CHUNKS = [(c, min(BANK, N_NODES - c)) for c in range(0, N_NODES, BANK)]
K8 = 8
BLOCKS = [(b, P, K8) for b in range(0, N_NODES - P * K8 + 1, P * K8)]
REST = N_NODES - len(BLOCKS) * P * K8
RK = 4
ZS = 4
BLOCKS.append((len(BLOCKS) * P * K8, REST // RK, RK))


def gnn_program(nc, x2T, src_cols, type_cols, dst_cols, dst_flat, weight_cols, basis2, compT,
                bias_col, res_wT, res_b_col, gamma_col, beta_col, out):
    f32, bf16, i32 = mybir.dt.float32, mybir.dt.bfloat16, mybir.dt.int32
    ALU, ACT, AX = mybir.AluOpType, mybir.ActivationFunctionType, mybir.AxisListType

    ctx = ExitStack()
    with ctx:
        def sb(name, shape, dt):
            return ctx.enter_context(nc.sbuf_tensor(name, shape, dt))

        def sem(name):
            return ctx.enter_context(nc.semaphore(name))

        table = nc.dram_tensor("message_table", [NODES_PADDED * RELS, F], f32).ap()
        table_tiles = table.rearrange("(t p r) o -> t p (r o)", p=P, r=RELS)
        base_dram = nc.dram_tensor("group_base", [GROUPS], i32).ap()
        span_dram = nc.dram_tensor("group_span", [GROUPS], i32).ap()

        xT = sb("xT", [P, NODES_PADDED], f32)
        h_arena = sb("h_arena", [P, H_COLUMNS], f32)
        hT = h_arena[0:F, :]
        basis_sb = h_arena[0:BASES, 0:2 * F * F].rearrange("b (o i) -> b o i", i=2 * F)
        w_f32 = h_arena[:, 2 * F * F:2 * F * F + ROW]
        y_stage = sb("y_stage", [P, 2 * UNITS * UNIT], f32)
        type_i = y_stage[:, 0:TILE_COLUMNS].bitcast(i32)
        dst_i = y_stage[:, TILE_COLUMNS:2 * TILE_COLUMNS].bitcast(i32)
        rows_at = 2 * TILE_COLUMNS
        dst_rows = y_stage[0:GP, rows_at:rows_at + GJ * GE].bitcast(i32)
        last_at = rows_at + GJ * GE
        dst_last = y_stage[0:1, last_at:last_at + LAST_EDGES].bitcast(i32)
        rem_at = last_at + LAST_EDGES
        w_rem = y_stage[:, rem_at:rem_at + UNIT]
        res_y = y_stage[0:F, 0:2 * BANK].rearrange("f (s n) -> f s n", s=2)
        z_buf = y_stage[:, 2 * BANK:6 * BANK].rearrange("p (s n) -> p s n", s=ZS)
        squares = y_stage[:, 6 * BANK:8 * BANK].rearrange("p (s n) -> p s n", s=2)

        w_high = sb("w_high", [P, ROW], bf16)
        w_mid = sb("w_mid", [P, ROW], bf16)
        w_lowhigh = sb("w_lowhigh", [P, ROW], bf16)
        x_hm = sb("x_hm", [P, 2, P], bf16)
        x_hl = sb("x_hl", [P, 2, P], bf16)
        x_rem = sb("x_rem", [P, 2, P], f32)

        row_index = sb("row_index", [P, TILE_COLUMNS], i32)
        dst_key = sb("dst_key", [P, TILE_COLUMNS], f32)
        weight = sb("weight", [P, TILE_COLUMNS], f32)
        base_row = sb("base_row", [P, GROUPS], i32)
        span_row = sb("span_row", [1, GROUPS], i32)
        span_max = sb("span_max", [1, 1], i32)
        base_g = sb("base_g", [GP, GJ], i32)
        span_g = sb("span_g", [GP, GJ], i32)
        last_bs = sb("last_bs", [1, 2], i32)
        comp_sb = sb("comp_sb", [BASES, RELS], f32)
        cols = sb("cols", [F, 4], f32)
        res_w = sb("res_w", [P, F], f32)

        index_slot = sb("index_slot", [P, SLOTS], i32)
        gathered_rows = sb("gathered_rows", [P, SLOTS, F], f32)
        node_iota = sb("node_iota", [P, WIDE], f32)
        wide_iota = sb("wide_iota", [P, WIDE], f32)
        select = sb("select", [P, 2, GROUP, WINDOW], f32)
        wide_select = sb("wide_select", [P, GROUP, WIDE], f32)

        stats = sb("stats", [F, len(CHUNKS), 6], f32)
        mv = sb("mv", [F, 2], f32)
        affine = sb("affine", [F, 6], f32)
        identity = sb("identity", [F, F], f32)
        combine = sb("combine", [P, F], f32)
        shift_diag = sb("shift_diag", [F, F], f32)
        ones = sb("ones", [F, P], f32)
        shift_row = sb("shift_row", [P, F], f32)
        eps_col = sb("eps_col", [P, 1], f32)
        shift_mean = sb("shift_mean", [P, 1], f32)
        deviation = sb("deviation", [P, ZS, 2, K8], f32)

        psum = ctx.enter_context(nc.psum_tensor("psum", [P, 8 * BANK], f32))

        wait_carrier = sem("wait_carrier")
        s_x = sem("s_x")
        s_basis = sem("s_basis")
        s_comp = sem("s_comp")
        s_edges = sem("s_edges")
        s_weight = sem("s_weight")
        s_rows = sem("s_rows")
        s_cols = sem("s_cols")
        s_resw = sem("s_resw")
        bases_found = sem("bases_found")
        bases_stored = sem("bases_stored")
        bases_loaded = sem("bases_loaded")
        flag_ready = sem("flag_ready")
        w_product = sem("w_product")
        w_copied = sem("w_copied")
        w_parts = sem("w_parts")
        x_parts = sem("x_parts")
        x_step = sem("x_step")
        unit_full = sem("unit_full")
        act_free = sem("act_free")
        dve_free = sem("dve_free")
        dve_step = sem("dve_step")
        stored = [sem(f"stored_{s}") for s in range(2 * UNITS)]
        edges_used = sem("edges_used")
        h_zeroed = sem("h_zeroed")
        key_shifted = sem("key_shifted")
        iota_step = sem("iota_step")
        constants = sem("constants")
        index_ready = sem("index_ready")
        gathered = [sem(f"gathered_{s}") for s in range(SLOTS)]
        select_ready = sem("select_ready")
        window_summed = sem("window_summed")
        sum_free = sem("sum_free")
        h_done = sem("h_done")
        res_product = sem("res_product")
        res_ready = sem("res_ready")
        relu_ready = sem("relu_ready")
        y_ready = sem("y_ready")
        stats_ready = sem("stats_ready")
        bn_step = sem("bn_step")
        shift_product = sem("shift_product")
        shift_step = sem("shift_step")
        z_product = sem("z_product")
        z_shifted = sem("z_shifted")
        z_squared = sem("z_squared")
        var_ready = sem("var_ready")
        std_ready = sem("std_ready")
        inverse_ready = sem("inverse_ready")
        z_ready = sem("z_ready")
        z_stored = [sem(f"z_stored_{s}") for s in range(ZS)]

        block = ctx.enter_context(nc.Block())

        def unit_psum(u):
            return psum[:, u * UNIT:(u + 1) * UNIT]

        def stage(t, u):
            s = (t % 2) * UNITS + u
            return y_stage[:, s * UNIT:(s + 1) * UNIT]

        @block.sync
        def _(sp):
            sp.dma_start(basis_sb, basis2).then_inc(s_basis, 16)
            sp.dma_start(comp_sb[:, :], compT).then_inc(s_comp, 16)
            sp.dma_start(dst_rows, dst_flat[0:GP * GJ * GE].rearrange("(p n) -> p n", p=GP)).then_inc(s_rows, 16)
            sp.dma_start(dst_last, dst_flat[GP * GJ * GE:N_EDGES].unsqueeze(0)).then_inc(s_rows, 16)
            sp.dma_start(xT[:, :], x2T).then_inc(s_x, 16)
            sp.wait_ge(bases_found, 1)
            sp.dma_start(base_dram[0:GP * GJ].rearrange("(p n) -> p n", p=GP), base_g[:, :]).then_inc(bases_stored, 16)
            sp.dma_start(span_dram[0:GP * GJ].rearrange("(p n) -> p n", p=GP), span_g[:, :]).then_inc(bases_stored, 16)
            sp.dma_start(base_dram[GP * GJ:GROUPS].unsqueeze(0), last_bs[:, 0:1]).then_inc(bases_stored, 16)
            sp.dma_start(span_dram[GP * GJ:GROUPS].unsqueeze(0), last_bs[:, 1:2]).then_inc(bases_stored, 16)
            sp.wait_ge(bases_stored, 64)
            sp.dma_start(base_row[:, :], base_dram.partition_broadcast(P)).then_inc(bases_loaded, 16)
            sp.dma_start(span_row[:, :], span_dram.unsqueeze(0)).then_inc(bases_loaded, 16)
            with sp.Fori(0, NODE_TILES // 2) as i:
                for t in range(2):
                    for u in range(UNITS):
                        sp.wait_ge(act_free if u % 2 == 0 else dve_free, 4 * i + 2 * t + u // 2 + 3)
                        sp.dma_start(table_tiles[2 * i + t, :, u * UNIT:(u + 1) * UNIT],
                                     stage(t, u)).then_inc(stored[t * UNITS + u], 16)
            for b, (n0, m, k) in enumerate(BLOCKS):
                sp.wait_ge(z_ready, b + 1)
                sp.dma_start(out[n0:n0 + m * k, :].rearrange("(p k) f -> p (k f)", k=k),
                             z_buf[0:m, b % ZS, 0:k * F]).then_inc(z_stored[b % ZS], 16)
            for s in range(ZS):
                sp.wait_ge(z_stored[s], 16 * len(range(s, len(BLOCKS), ZS)))

        @block.gpsimd
        def _(pool):
            nc.gpsimd.iota(node_iota[:, :], [[1, WIDE]], base=0, channel_multiplier=0,
                           allow_small_or_imprecise_dtypes=True).then_inc(constants, 1)
            nc.gpsimd.memset(combine[:, :], 0.0).then_inc(constants, 1)
            nc.gpsimd.memset(identity[:, :], 0.0).then_inc(constants, 1)
            nc.gpsimd.memset(ones[:, :], 1.0).then_inc(constants, 1)
            nc.gpsimd.memset(eps_col[:, :], BN_EPS).then_inc(constants, 1)
            pool.wait_ge(constants, 6)
            nc.gpsimd.affine_select(out=identity[:, :], in_=identity[:, :], compare_op=ALU.not_equal, fill=1.0,
                                    base=0, pattern=[[-1, F]], channel_multiplier=1).then_inc(constants, 1)
            nc.gpsimd.affine_select(out=combine[:, :], in_=combine[:, :], compare_op=ALU.not_equal, fill=1.0,
                                    base=-F, pattern=[[-1, F]], channel_multiplier=1).then_inc(constants, 1)
            pool.wait_ge(s_x, 16)

            def split_x(i, t):
                x_tile = bass.ds((2 * i + t) * P, P)
                done = 2 * i + t
                nc.gpsimd.tensor_copy(x_hm[:, t, :], xT[:, x_tile]).then_inc(x_step, 1)
                nc.gpsimd.tensor_copy(x_hl[:, t, :], xT[:, x_tile]).then_inc(x_step, 1)
                pool.wait_ge(x_step, 4 * done + 2)
                nc.gpsimd.tensor_tensor(x_rem[F:P, t, :], xT[F:P, x_tile], x_hl[F:P, t, :],
                                        ALU.subtract).then_inc(x_step, 1)
                pool.wait_ge(x_step, 4 * done + 3)
                pool.sem_inc(wait_carrier, 1)
                nc.gpsimd.tensor_copy(x_hm[F:P, t, :], x_rem[F:P, t, :]).then_inc(x_step, 1)
                pool.wait_ge(x_step, 4 * done + 4)
                nc.gpsimd.tensor_tensor(x_hl[F:P, t, :], x_rem[F:P, t, :], x_hm[F:P, t, :],
                                        ALU.subtract).then_inc(x_parts, 1)

            split_x(0, 0)
            pool.wait_ge(x_parts, 1)
            split_x(0, 1)
            with pool.Fori(1, NODE_TILES // 2) as i:
                for t in range(2):
                    pool.wait_ge(unit_full, UNITS * (2 * i + t - 1))
                    pool.wait_ge(x_parts, 2 * i + t)
                    pool.sem_inc(wait_carrier, 1)
                    split_x(i, t)
            pool.wait_ge(w_parts, UNITS)
            nc.gpsimd.memset(hT, 0.0).then_inc(h_zeroed, 1)
            for s in range(2 * UNITS):
                pool.wait_ge(stored[s], 16 * (NODE_TILES // 2))

            def gather(slot, rows=P):
                pool.indirect_dma_start(
                    out=gathered_rows[0:rows, slot, :], out_offset=None, in_=table,
                    in_offset=bass.IndirectOffsetOnAxis(ap=index_slot[0:rows, slot:slot + 1], axis=0),
                ).then_inc(gathered[slot], 16)

            with pool.Fori(0, TURNS) as i:
                for q in range(QUADS):
                    pool.wait_ge(index_ready, QUADS * i + q + 1)
                    pool.sem_inc(wait_carrier, 1)
                    for k in range(GROUP):
                        gather(q * GROUP + k)
            for g in range(TURNS * QUADS, GROUPS):
                q = g % QUADS
                pool.wait_ge(index_ready, g + 1)
                for k in range(GROUP):
                    tile = g * GROUP + k
                    if tile < EDGE_TILES:
                        gather(q * GROUP + k, P if tile < EDGE_TILES - 1 else LAST_TILE_ROWS)

        @block.tensor
        def _(pe):
            pe.wait_ge(s_basis, 16)
            pe.wait_ge(s_comp, 16)
            for o in range(F):
                last = nc.tensor.matmul(psum[:, o * RELS:(o + 1) * RELS], basis_sb[:, o, :], comp_sb[:, :],
                                        start=True, stop=True)
            last.then_inc(w_product, 1)
            pe.wait_ge(w_copied, 2)
            with pe.Fori(0, NODE_TILES // 2) as i:
                for t in range(2):
                    pe.wait_ge(x_parts, 2 * i + t + 1)
                    for u in range(UNITS):
                        pe.wait_ge(w_parts, u + 1)
                        pe.wait_ge(act_free if u % 2 == 0 else dve_free, 4 * i + 2 * t + u // 2 + 1)
                        for c in range(2 * u, 2 * u + 2):
                            at = slice(c * BANK, (c + 1) * BANK)
                            nc.tensor.matmul(psum[:, at], x_hl[:, t, :], w_lowhigh[:, at], start=True, stop=False)
                            nc.tensor.matmul(psum[:, at], x_hm[:, t, :], w_mid[:, at], start=False, stop=False)
                            last = nc.tensor.matmul(psum[:, at], x_hm[:, t, :], w_high[:, at], start=False, stop=True)
                        last.then_inc(unit_full, 1)
            pe.wait_ge(act_free, 2 * NODE_TILES + 2)
            pe.wait_ge(dve_free, 2 * NODE_TILES + 2)

            def sum_group(q, turn, rhs, width, ready, free, tiles=GROUP, last_rows=P):
                pe.wait_ge(select_ready, ready)
                pe.wait_ge(sum_free, free)
                for k in range(tiles):
                    slot = q * GROUP + k
                    rows = last_rows if k == tiles - 1 else P
                    pe.wait_ge(gathered[slot], 16 * (turn + 1))
                    last = nc.tensor.matmul(psum[0:F, q * BANK:q * BANK + width], gathered_rows[0:rows, slot, :],
                                            rhs(k, rows), start=(k == 0), stop=(k == tiles - 1))
                last.then_inc(window_summed, 1)

            def tail(g):
                tiles = min(GROUP, EDGE_TILES - g * GROUP)
                return dict(tiles=tiles, last_rows=LAST_TILE_ROWS if g == GROUPS - 1 else P)

            pe.wait_ge(flag_ready, 1)
            span = pe.value_load(span_max[0:1, 0:1], min_val=0, max_val=N_NODES)
            with pe.If(span < WINDOW):
                def narrow(q):
                    return lambda k, rows: select[0:rows, q % 2, k, :]

                with pe.Fori(0, TURNS) as i:
                    for q in range(QUADS):
                        n = QUADS * i + q + 1
                        sum_group(q, i, narrow(q), WINDOW, n, n)
                for g in range(TURNS * QUADS, GROUPS):
                    sum_group(g % QUADS, g // QUADS, narrow(g % QUADS), WINDOW, g + 1, g + 1, **tail(g))
            with pe.Else():
                def wide(k, rows):
                    return wide_select[0:rows, k, :]

                with pe.Fori(0, TURNS) as i:
                    for q in range(QUADS):
                        with pe.Fori(0, WIDE_WINDOWS) as w:
                            n = (QUADS * i + q) * WIDE_WINDOWS + w + 1
                            sum_group(q, i, wide, WIDE, n, n + QUADS - 1)
                for g in range(TURNS * QUADS, GROUPS):
                    with pe.Fori(0, WIDE_WINDOWS) as w:
                        n = g * WIDE_WINDOWS + w + 1
                        sum_group(g % QUADS, g // QUADS, wide, WIDE, n, n + QUADS - 1, **tail(g))
            pe.wait_ge(h_done, 1)
            pe.wait_ge(s_resw, 16)
            pe.wait_ge(constants, 8)
            for c, (c0, m) in enumerate(CHUNKS):
                if c >= 2:
                    pe.wait_ge(res_ready, c - 1)
                nc.tensor.matmul(psum[0:F, (4 + c % 2) * BANK:(4 + c % 2) * BANK + m], res_w[:, :], xT[:, c0:c0 + m],
                                 start=True, stop=True).then_inc(res_product, 1)
            pe.wait_ge(bn_step, BN_STEPS)
            nc.tensor.matmul(psum[:, 0:F], ones[:, :], shift_diag[:, :], start=True, stop=True).then_inc(shift_product, 1)
            pe.wait_ge(res_ready, len(CHUNKS))
            for b, (n0, m, k) in enumerate(BLOCKS):
                if b >= 2:
                    pe.wait_ge(z_shifted, b - 1)
                for j in range(k):
                    at = (4 + b % 2) * BANK + j * F
                    last = nc.tensor.matmul(psum[0:m, at:at + F], xT[:, n0 + j:n0 + j + (m - 1) * k + 1:k],
                                            combine[:, :], start=True, stop=True)
                last.then_inc(z_product, 1)

        @block.scalar
        def _(act):
            act.dma_start(row_index[:, :], src_cols).then_inc(s_edges, 16)
            act.dma_start(type_i, type_cols).then_inc(s_edges, 16)
            act.dma_start(dst_i, dst_cols).then_inc(s_edges, 16)
            act.dma_start(weight[:, :], weight_cols).then_inc(s_weight, 16)
            act.dma_start(cols[:, 0:1], bias_col).then_inc(s_cols, 16)
            act.dma_start(cols[:, 1:2], res_b_col).then_inc(s_cols, 16)
            act.dma_start(cols[:, 2:3], gamma_col).then_inc(s_cols, 16)
            act.dma_start(cols[:, 3:4], beta_col).then_inc(s_cols, 16)
            act.dma_start(res_w[0:F, :], res_wT).then_inc(s_resw, 16)
            act.wait_ge(w_product, 1)
            w_out = w_f32.rearrange("p (r o) -> p o r", o=F)
            w_in = psum[:, :].rearrange("p (o r) -> p o r", r=RELS)
            nc.scalar.copy(w_out[:, 0:F // 2, :], w_in[:, 0:F // 2, :]).then_inc(w_copied, 1)
            act.wait_ge(w_copied, 2)
            act.sem_inc(act_free, 2)
            act.wait_ge(edges_used, 1)
            for peeled in (True, False):
                def evacuate(i):
                    for t in range(2):
                        for u in range(0, UNITS, 2):
                            act.wait_ge(unit_full, UNITS * (2 * i + t) + u + 1)
                            if not peeled:
                                act.wait_ge(stored[t * UNITS + u], 16 * i)
                            nc.scalar.copy(stage(t, u), unit_psum(u)).then_inc(act_free, 1)
                if peeled:
                    evacuate(0)
                else:
                    with act.Fori(1, NODE_TILES // 2) as i:
                        evacuate(i)
            act.wait_ge(s_cols, 64)
            act.wait_ge(h_done, 1)
            for c, (c0, m) in enumerate(CHUNKS):
                nc.scalar.activation(hT[:, c0:c0 + m], hT[:, c0:c0 + m], ACT.Relu,
                                     bias=cols[:, 0:1]).then_inc(relu_ready, 1)
                act.wait_ge(res_product, c + 1)
                if c >= 2:
                    act.wait_ge(y_ready, c - 1)
                nc.scalar.activation(res_y[:, c % 2, 0:m], psum[0:F, (4 + c % 2) * BANK:(4 + c % 2) * BANK + m],
                                     ACT.Relu, bias=cols[:, 1:2]).then_inc(res_ready, 1)
            act.wait_ge(bn_step, 1)
            nc.scalar.activation(affine[:, 0:1], mv[:, 1:2], ACT.Sqrt, bias=eps_col[0:F, :]).then_inc(bn_step, 1)
            for b in range(len(BLOCKS) + 1):
                if b < len(BLOCKS):
                    _, m, k = BLOCKS[b]
                    act.wait_ge(z_shifted, b + 1)
                    if b >= 2:
                        act.wait_ge(var_ready, b - 1)
                    nc.scalar.activation(squares[0:m, b % 2, 0:k * F], z_buf[0:m, b % ZS, 0:k * F],
                                         ACT.Square).then_inc(z_squared, 1)
                if b >= 1:
                    _, m, k = BLOCKS[b - 1]
                    act.wait_ge(var_ready, b)
                    sums = deviation[0:m, (b - 1) % ZS, 0, 0:k]
                    nc.scalar.activation(sums, sums, ACT.Sqrt, bias=eps_col[0:m, :],
                                         scale=1.0 / F).then_inc(std_ready, 1)

        @block.vector
        def _(dve):
            steps = [0]

            def step(instruction):
                steps[0] += 1
                instruction.then_inc(dve_step, 1)
                dve.wait_ge(dve_step, steps[0])

            nc.vector.memset(res_w[F:P, :], 0.0).then_inc(constants, 1)
            dve.wait_ge(s_rows, 32)
            grouped = dst_rows.rearrange("p (g e) -> p g e", g=GJ)
            nc.vector.tensor_reduce(base_g[:, :], grouped, AX.X, ALU.min).then_inc(dve_step, 1)
            nc.vector.tensor_reduce(span_g[:, :], grouped, AX.X, ALU.max).then_inc(dve_step, 1)
            nc.vector.tensor_reduce(last_bs[:, 0:1], dst_last, AX.X, ALU.min).then_inc(dve_step, 1)
            nc.vector.tensor_reduce(last_bs[:, 1:2], dst_last, AX.X, ALU.max).then_inc(dve_step, 1)
            steps[0] = 4
            dve.wait_ge(dve_step, 4)
            step(nc.vector.tensor_tensor(span_g[:, :], span_g[:, :], base_g[:, :], ALU.subtract))
            nc.vector.tensor_tensor(last_bs[:, 1:2], last_bs[:, 1:2], last_bs[:, 0:1], ALU.subtract).then_inc(bases_found, 1)
            dve.wait_ge(s_edges, 48)
            step(nc.vector.scalar_tensor_tensor(out=row_index[:, :], in0=row_index[:, :], scalar=float(RELS),
                                                in1=type_i, op0=ALU.mult, op1=ALU.add))
            dve.wait_ge(w_product, 1)
            w_out = w_f32.rearrange("p (r o) -> p o r", o=F)
            w_in = psum[:, :].rearrange("p (o r) -> p o r", r=RELS)
            nc.vector.tensor_copy(w_out[:, F // 2:F, :], w_in[:, F // 2:F, :]).then_inc(w_copied, 1)
            dve.wait_ge(w_copied, 2)
            dve.sem_inc(dve_free, 2)
            for u in range(UNITS):
                at = slice(u * UNIT, (u + 1) * UNIT)
                step(nc.vector.tensor_copy(w_high[:, at], w_f32[:, at]))
                nc.vector.tensor_copy(w_lowhigh[F:P, at], w_high[F:P, at]).then_inc(dve_step, 1)
                steps[0] += 1
                step(nc.vector.tensor_tensor(w_rem, w_f32[:, at], w_high[:, at], ALU.subtract))
                step(nc.vector.tensor_copy(w_mid[:, at], w_rem))
                nc.vector.tensor_tensor(w_lowhigh[0:F, at], w_rem[0:F, :], w_mid[0:F, at],
                                        ALU.subtract).then_inc(w_parts, 1)
                dve.wait_ge(w_parts, u + 1)
            dve.wait_ge(bases_loaded, 32)
            step(nc.vector.tensor_reduce(span_max[:, :], span_row[:, :], AX.X, ALU.max))
            step(nc.vector.tensor_copy(dst_key[:, :], dst_i))
            dve.sem_inc(edges_used, 1)
            for peeled in (True, False):
                def evacuate(i):
                    for t in range(2):
                        for u in range(1, UNITS, 2):
                            dve.wait_ge(unit_full, UNITS * (2 * i + t) + u + 1)
                            if not peeled:
                                dve.wait_ge(stored[t * UNITS + u], 16 * i)
                            nc.vector.tensor_copy(stage(t, u), unit_psum(u)).then_inc(dve_free, 1)
                if peeled:
                    evacuate(0)
                else:
                    with dve.Fori(1, NODE_TILES // 2) as i:
                        evacuate(i)

            def indices(g, q):
                slots = slice(q * GROUP, (q + 1) * GROUP)
                nc.vector.tensor_copy(index_slot[:, slots], row_index[:, bass.ds(g * GROUP, GROUP)]
                                      ).then_inc(index_ready, 1)

            for q in range(QUADS):
                indices(q, q)
            dve.sem_inc(sum_free, QUADS)
            dve.sem_inc(flag_ready, 1)
            dve.wait_ge(constants, 8)
            dve.wait_ge(s_weight, 16)
            dve.wait_ge(h_zeroed, 1)
            span = dve.value_load(span_max[0:1, 0:1], min_val=0, max_val=N_NODES)
            with dve.If(span < WINDOW):
                whole = dst_key[:, 0:GROUPS * GROUP].rearrange("p (g k) -> p g k", k=GROUP)
                nc.vector.tensor_tensor(whole, whole, base_row[:, :].unsqueeze(2).broadcast_to([P, GROUPS, GROUP]),
                                        ALU.subtract).then_inc(key_shifted, 1)
                dve.wait_ge(key_shifted, 1)

                def selection(g, s):
                    for k in range(GROUP):
                        t = g * GROUP + k
                        last = nc.vector.tensor_scalar(select[:, s, k, :], node_iota[:, 0:WINDOW],
                                                       dst_key[:, bass.ds(t, 1)], weight[:, bass.ds(t, 1)],
                                                       ALU.is_equal, ALU.mult)
                    last.then_inc(select_ready, 1)

                def add_window(g, q):
                    base = dve.value_load(base_row[0:1, bass.ds(g, 1)], min_val=0, max_val=N_NODES - 1)
                    window = hT[:, bass.ds(base, WINDOW)]
                    dve.wait_ge(sum_free, g + QUADS)
                    nc.vector.tensor_tensor(window, window, psum[0:F, q * BANK:q * BANK + WINDOW],
                                            ALU.add).then_inc(sum_free, 1)

                selection(0, 0)
                with dve.Fori(0, TURNS) as i:
                    for q in range(QUADS):
                        g = QUADS * i + q
                        selection(g + 1, (q + 1) % 2)
                        dve.wait_ge(window_summed, g + 1)
                        indices(g + QUADS, q)
                        add_window(g, q)
                for g in range(TURNS * QUADS, GROUPS):
                    if g + 1 < GROUPS:
                        selection(g + 1, (g + 1) % 2)
                    dve.wait_ge(window_summed, g + 1)
                    add_window(g, g % QUADS)
                dve.wait_ge(sum_free, GROUPS + QUADS)
            with dve.Else():
                def add_wide(g, q, w):
                    n = g * WIDE_WINDOWS + w
                    for k in range(GROUP):
                        t = g * GROUP + k
                        last = nc.vector.tensor_scalar(wide_select[:, k, :], wide_iota[:, :],
                                                       dst_key[:, bass.ds(t, 1)], weight[:, bass.ds(t, 1)],
                                                       ALU.is_equal, ALU.mult)
                    last.then_inc(select_ready, 1)
                    dve.wait_ge(window_summed, n + 1)
                    window = hT[:, bass.ds(w * WIDE, WIDE)]
                    nc.vector.tensor_tensor(window, window, psum[0:F, q * BANK:(q + 1) * BANK],
                                            ALU.add).then_inc(sum_free, 1)
                    dve.wait_ge(sum_free, n + 1 + QUADS)
                    nc.vector.tensor_scalar(wide_iota[:, :], wide_iota[:, :], float(WIDE), None,
                                            ALU.add).then_inc(iota_step, 1)
                    dve.wait_ge(iota_step, n + g + 2)

                def group(g, q):
                    nc.vector.tensor_copy(wide_iota[:, :], node_iota[:, :]).then_inc(iota_step, 1)
                    dve.wait_ge(iota_step, g * (WIDE_WINDOWS + 1) + 1)
                    dve.sem_inc(wait_carrier, 1)
                    with dve.Fori(0, WIDE_WINDOWS) as w:
                        add_wide(g, q, w)

                with dve.Fori(0, TURNS) as i:
                    for q in range(QUADS):
                        group(QUADS * i + q, q)
                        indices(QUADS * i + q + QUADS, q)
                for g in range(TURNS * QUADS, GROUPS):
                    group(g, g % QUADS)
            dve.sem_inc(h_done, 1)

            for c, (c0, m) in enumerate(CHUNKS):
                dve.wait_ge(relu_ready, c + 1)
                dve.wait_ge(res_ready, c + 1)
                nc.vector.tensor_tensor(xT[0:F, c0:c0 + m], hT[:, c0:c0 + m], res_y[:, c % 2, 0:m],
                                        ALU.add).then_inc(y_ready, 1)
                dve.wait_ge(y_ready, c + 1)
                nc.vector.bn_stats(stats[:, c, :], xT[0:F, c0:c0 + m]).then_inc(stats_ready, 1)
            dve.wait_ge(stats_ready, len(CHUNKS))
            nc.vector.bn_aggr(mv[:, :], stats[:, :, :].rearrange("f c s -> f (c s)")).then_inc(bn_step, 1)
            dve.wait_ge(bn_step, 2)
            nc.vector.reciprocal(affine[:, 1:2], affine[:, 0:1]).then_inc(bn_step, 1)
            dve.wait_ge(bn_step, 3)
            nc.vector.tensor_tensor(affine[:, 2:3], affine[:, 1:2], cols[:, 2:3], ALU.mult).then_inc(bn_step, 1)
            dve.wait_ge(bn_step, 4)
            nc.vector.tensor_tensor(affine[:, 3:4], mv[:, 0:1], affine[:, 2:3], ALU.mult).then_inc(bn_step, 1)
            nc.vector.tensor_scalar(affine[:, 5:6], affine[:, 2:3], 1.0 / F, None, ALU.mult).then_inc(bn_step, 1)
            dve.wait_ge(bn_step, 6)
            nc.vector.tensor_tensor(affine[:, 4:5], cols[:, 3:4], affine[:, 3:4], ALU.subtract).then_inc(bn_step, 1)
            dve.wait_ge(bn_step, 7)
            nc.vector.tensor_scalar(shift_diag[:, :], identity[:, :], affine[:, 4:5], None,
                                    ALU.mult).then_inc(bn_step, 1)
            nc.vector.tensor_scalar(combine[0:F, :], identity[:, :], affine[:, 2:3], affine[:, 5:6],
                                    ALU.mult, ALU.subtract).then_inc(bn_step, 1)
            nc.vector.tensor_scalar(combine[F:P, :], combine[F:P, :], 1.0 / F, None,
                                    ALU.subtract).then_inc(bn_step, 1)
            dve.wait_ge(shift_product, 1)
            nc.vector.tensor_reduce(shift_mean[:, :], psum[:, 0:F], AX.X, ALU.add).then_inc(shift_step, 1)
            dve.wait_ge(shift_step, 1)
            nc.vector.tensor_scalar(shift_mean[:, :], shift_mean[:, :], 1.0 / F, None, ALU.mult).then_inc(shift_step, 1)
            dve.wait_ge(shift_step, 2)
            nc.vector.tensor_scalar(shift_row[:, :], psum[:, 0:F], shift_mean[:, 0:1], None,
                                    ALU.subtract).then_inc(shift_step, 1)
            dve.wait_ge(shift_step, 3)
            for b in range(len(BLOCKS) + 2):
                if b < len(BLOCKS):
                    _, m, k = BLOCKS[b]
                    at = (4 + b % 2) * BANK
                    dve.wait_ge(z_product, b + 1)
                    if b >= ZS:
                        dve.wait_ge(z_stored[b % ZS], 16 * (b // ZS))
                    nc.vector.tensor_tensor(z_buf[0:m, b % ZS, 0:k * F].rearrange("p (k f) -> p k f", k=k),
                                            psum[0:m, at:at + k * F].rearrange("p (k f) -> p k f", k=k),
                                            shift_row[0:m, :].unsqueeze(1).broadcast_to([m, k, F]),
                                            ALU.add).then_inc(z_shifted, 1)
                if 1 <= b <= len(BLOCKS):
                    _, m, k = BLOCKS[b - 1]
                    dve.wait_ge(z_squared, b)
                    nc.vector.tensor_reduce(deviation[0:m, (b - 1) % ZS, 0, 0:k],
                                            squares[0:m, (b - 1) % 2, 0:k * F].rearrange("p (k f) -> p k f", k=k),
                                            AX.X, ALU.add).then_inc(var_ready, 1)
                if b >= 2:
                    _, m, k = BLOCKS[b - 2]
                    s = (b - 2) % ZS
                    dve.wait_ge(std_ready, b - 1)
                    nc.vector.reciprocal(deviation[0:m, s, 1, 0:k], deviation[0:m, s, 0, 0:k]).then_inc(inverse_ready, 1)
                    dve.wait_ge(inverse_ready, b - 1)
                    z = z_buf[0:m, s, 0:k * F].rearrange("p (k f) -> p k f", k=k)
                    nc.vector.tensor_tensor(z, z, deviation[0:m, s, 1, 0:k].unsqueeze(2).broadcast_to([m, k, F]),
                                            ALU.mult).then_inc(z_ready, 1)


def kernel(x, src, dst, edge_type_64, edge_weight1, L0_gnn_basis, L0_gnn_comp, L0_gnn_bias, L0_gnn_res_w,
           L0_gnn_res_b, L0_gnn_gamma, L0_gnn_beta):
    import numpy as np
    import concourse.bacc as bacc
    from concourse.bass_utils import run_bass_kernel_spmd

    def tile_columns(a):
        a = np.asarray(a).reshape(-1)
        padded = np.zeros(TILE_COLUMNS * P, a.dtype)
        padded[:N_EDGES] = a
        return np.ascontiguousarray(padded.reshape(TILE_COLUMNS, P).T)

    def column(a):
        return np.ascontiguousarray(np.asarray(a).reshape(F, 1))

    xT = np.zeros((F, NODES_PADDED), np.float32)
    xT[:, :N_NODES] = np.asarray(x).T
    basis = np.asarray(L0_gnn_basis).transpose(0, 2, 1)
    arrays = {
        "x2T": np.concatenate([xT, xT], axis=0),
        "src_cols": tile_columns(src),
        "type_cols": tile_columns(edge_type_64),
        "dst_cols": tile_columns(dst),
        "dst_flat": np.ascontiguousarray(np.asarray(dst)),
        "weight_cols": tile_columns(edge_weight1),
        "basis2": np.ascontiguousarray(np.concatenate([basis, basis], axis=2)),
        "compT": np.ascontiguousarray(np.asarray(L0_gnn_comp).T),
        "bias_col": column(L0_gnn_bias),
        "res_wT": np.ascontiguousarray(np.asarray(L0_gnn_res_w).T),
        "res_b_col": column(L0_gnn_res_b),
        "gamma_col": column(L0_gnn_gamma),
        "beta_col": column(L0_gnn_beta),
    }
    nc = bacc.Bacc("TRN2", target_bir_lowering=False, num_devices=1)
    args = {name: nc.dram_tensor(name, a.shape, mybir.dt.from_np(a.dtype), kind="ExternalInput").ap()
            for name, a in arrays.items()}
    out = nc.dram_tensor("out", (N_NODES, F), mybir.dt.float32, kind="ExternalOutput").ap()
    gnn_program(nc, out=out, **args)
    result = run_bass_kernel_spmd(nc, [arrays], core_ids=[0])
    return result.results[0]["out"]
```

```python
import concourse.bass as bass
from concourse import mybir
from contextlib import ExitStack

P = 128
N_NODES = 12500
N_EDGES = 200000
F = 64
RELS = 64
BASES = 64
BN_EPS = 1e-05
LN_EPS = 1e-05

NODE_TILES = -(-N_NODES // P)
NODES_PADDED = NODE_TILES * P
ROW = RELS * F
UNIT = 1024
UNITS = ROW // UNIT
BANK = 512

GROUP = 4
EDGE_TILES = -(-N_EDGES // P)
LAST_TILE_ROWS = N_EDGES - (EDGE_TILES - 1) * P
GROUPS = -(-EDGE_TILES // GROUP)
QUADS = 4
SLOTS = GROUP * QUADS
ALL_TURNS = GROUPS // QUADS
TILE_COLUMNS = (GROUPS + QUADS - 1) * GROUP

PAIR = 2
DIRECT_PER_TURN = PAIR * QUADS
TURNS = EDGE_TILES // (SLOTS + DIRECT_PER_TURN)
DIRECT_TILES = TURNS * DIRECT_PER_TURN
FIRST_GROUP = DIRECT_TILES // GROUP
RING = 4
BEHIND = 2
assert DIRECT_TILES % GROUP == 0 and TURNS % RING == 1
assert 0 <= GROUPS - FIRST_GROUP - TURNS * QUADS < QUADS

WINDOW = 128
NARROW = 8
KEYS = NARROW * RELS
REL_PAIRS = RELS // 2
WIDE = 512
WIDE_WINDOWS = -(-N_NODES // WIDE)
H_COLUMNS = max(WIDE_WINDOWS * WIDE, N_NODES + WINDOW)

GP = 78
GJ = (GROUPS - 1) // GP
GE = GROUP * P
LAST_EDGES = N_EDGES - (GROUPS - 1) * GE

BN_STEPS = 10
CHUNKS = [(c, min(BANK, N_NODES - c)) for c in range(0, N_NODES, BANK)]
K8 = 8
BLOCKS = [(b, P, K8) for b in range(0, N_NODES - P * K8 + 1, P * K8)]
REST = N_NODES - len(BLOCKS) * P * K8
RK = 4
ZS = 4
BLOCKS.append((len(BLOCKS) * P * K8, REST // RK, RK))


def gnn_program(nc, x_rows, x2T, src_cols, type_cols, dst_cols, dst_flat, weight_cols, basis2, compT,
                bias_col, res_wT, res_b_col, gamma_col, beta_col, out):
    f32, bf16, i32 = mybir.dt.float32, mybir.dt.bfloat16, mybir.dt.int32
    ALU, ACT, AX = mybir.AluOpType, mybir.ActivationFunctionType, mybir.AxisListType

    ctx = ExitStack()
    with ctx:
        def sb(name, shape, dt):
            return ctx.enter_context(nc.sbuf_tensor(name, shape, dt))

        def sem(name):
            return ctx.enter_context(nc.semaphore(name))

        table = nc.dram_tensor("message_table", [NODES_PADDED * RELS, F], f32).ap()
        table_tiles = table.rearrange("(t p r) o -> t p (r o)", p=P, r=RELS)
        base_dram = nc.dram_tensor("group_base", [GROUPS], i32).ap()
        span_dram = nc.dram_tensor("group_span", [GROUPS], i32).ap()
        direct_base_dram = nc.dram_tensor("direct_base", [DIRECT_TILES], i32).ap()
        direct_span_dram = nc.dram_tensor("direct_span", [DIRECT_TILES], i32).ap()
        x_direct = nc.dram_tensor("x_direct", [TURNS, P, DIRECT_PER_TURN * F], f32).ap()

        xT = sb("xT", [P, NODES_PADDED], f32)
        h_arena = sb("h_arena", [P, H_COLUMNS], f32)
        hT = h_arena[0:F, :]
        basis_sb = h_arena[0:BASES, 0:2 * F * F].rearrange("b (o i) -> b o i", i=2 * F)
        w_f32 = h_arena[:, 2 * F * F:2 * F * F + ROW]
        y_stage = sb("y_stage", [P, 2 * UNITS * UNIT], f32)
        type_i = y_stage[:, 0:TILE_COLUMNS].bitcast(i32)
        dst_i = y_stage[:, TILE_COLUMNS:2 * TILE_COLUMNS].bitcast(i32)
        rows_at = 2 * TILE_COLUMNS
        dst_rows = y_stage[0:GP, rows_at:rows_at + GJ * GE].bitcast(i32)
        last_at = rows_at + GJ * GE
        dst_last = y_stage[0:1, last_at:last_at + LAST_EDGES].bitcast(i32)
        direct_at = last_at + LAST_EDGES
        dst_direct = y_stage[0:TURNS, direct_at:direct_at + DIRECT_PER_TURN * P].bitcast(i32)
        direct_rows = h_arena[:, UNIT:UNIT + RING * DIRECT_PER_TURN * F].rearrange(
            "p (s k f) -> p s k f", s=RING, k=DIRECT_PER_TURN)
        w_rem = h_arena[:, 0:UNIT]
        pair_sums = y_stage[:, 0:REL_PAIRS * 64].rearrange("p (r c) -> p r c", r=REL_PAIRS)
        select = y_stage[:, 2048:3072].rearrange("p (s k n) -> p s k n", s=2, k=GROUP)
        pair_select = y_stage[:, 3072:4096].bitcast(bf16).rearrange("p (s j c) -> p s j c", s=2, j=PAIR)
        direct_x = y_stage[:, 4096:4608].rearrange("p (q c) -> p q c", q=QUADS)
        scaled = y_stage[:, 4608:4864].rearrange("p (s c) -> p s c", s=2)
        scaled_rem = y_stage[:, 4864:5120].rearrange("p (s c) -> p s c", s=2)
        parts = y_stage[:, 5120:5504].bitcast(bf16).rearrange("p (t s c) -> p t s c", t=3, s=2)
        res_y = y_stage[0:F, 0:2 * BANK].rearrange("f (s n) -> f s n", s=2)
        z_buf = y_stage[:, 2 * BANK:6 * BANK].rearrange("p (s n) -> p s n", s=ZS)
        squares = y_stage[:, 6 * BANK:8 * BANK].rearrange("p (s n) -> p s n", s=2)

        stats = y_stage[0:F, 8 * BANK:8 * BANK + 6 * len(CHUNKS)].rearrange("f (c s) -> f c s", s=6)
        shift_row = y_stage[:, 9 * BANK:9 * BANK + F]
        shift_diag = y_stage[0:F, 9 * BANK + F:9 * BANK + 2 * F]

        w_high = sb("w_high", [P, ROW], bf16)
        w_mid = sb("w_mid", [P, ROW], bf16)
        w_lowhigh = sb("w_lowhigh", [P, ROW], bf16)
        wide_select = w_high[:, :].bitcast(f32).rearrange("p (k n) -> p k n", k=GROUP)
        wide_iota = w_mid[:, 0:2 * WIDE].bitcast(f32)
        w_pairs = sb("w_pairs", [P, REL_PAIRS, F], f32)
        x_hm = sb("x_hm", [P, 2, P], bf16)
        x_hl = sb("x_hl", [P, 2, P], bf16)
        x_rem = sb("x_rem", [P, 2, P], f32)

        row_index = sb("row_index", [P, TILE_COLUMNS], i32)
        dst_key = sb("dst_key", [P, TILE_COLUMNS], f32)
        weight = sb("weight", [P, TILE_COLUMNS], f32)
        gathered_rows = sb("gathered_rows", [P, SLOTS, F], f32)
        base_row = sb("base_row", [P, GROUPS], i32)
        span_row = sb("span_row", [1, GROUPS], i32)
        direct_src = sb("direct_src", [P, DIRECT_TILES], i32)
        direct_key = sb("direct_key", [P, DIRECT_TILES], f32)
        direct_base_row = sb("direct_base_row", [P, DIRECT_TILES], i32)
        direct_span_row = sb("direct_span_row", [1, DIRECT_TILES], i32)
        span_max = sb("span_max", [1, 2], i32)
        relative = h_arena[:, 0:DIRECT_TILES]
        base_g = sb("base_g", [GP, GJ], i32)
        span_g = sb("span_g", [GP, GJ], i32)
        last_bs = sb("last_bs", [1, 2], i32)
        base_d = sb("base_d", [TURNS, DIRECT_PER_TURN], i32)
        span_d = sb("span_d", [TURNS, DIRECT_PER_TURN], i32)
        direct_index = sb("direct_index", [P, RING, DIRECT_PER_TURN], i32)
        comp_sb = sb("comp_sb", [BASES, RELS], f32)
        cols = sb("cols", [F, 4], f32)
        res_w = sb("res_w", [P, F], f32)

        index_slot = sb("index_slot", [P, SLOTS], i32)
        node_iota = sb("node_iota", [P, WIDE], f32)
        key_iota = sb("key_iota", [P, KEYS], f32)

        mv = sb("mv", [F, 2], f32)
        affine = sb("affine", [F, 6], f32)
        identity = sb("identity", [F, F], f32)
        combine = sb("combine", [P, F], f32)
        ones = sb("ones", [F, P], f32)
        eps_col = sb("eps_col", [P, 1], f32)
        shift_mean = sb("shift_mean", [P, 1], f32)
        deviation = sb("deviation", [P, ZS, 2, K8], f32)

        psum = ctx.enter_context(nc.psum_tensor("psum", [P, 8 * BANK], f32))

        wait_carrier = sem("wait_carrier")
        s_x = sem("s_x")
        s_basis = sem("s_basis")
        s_comp = sem("s_comp")
        s_x_rest = sem("s_x_rest")
        s_edges = sem("s_edges")
        s_direct_src = sem("s_direct_src")
        direct_copied = sem("direct_copied")
        direct_gathered = [sem(f"direct_gathered_{s}") for s in range(RING * DIRECT_PER_TURN)]
        direct_stored = [sem(f"direct_stored_{s}") for s in range(RING)]
        direct_loaded = [sem(f"direct_loaded_{q}") for q in range(QUADS)]
        pair_scaled = sem("pair_scaled")
        pair_selected = sem("pair_selected")
        pair_high = sem("pair_high")
        pair_rem = sem("pair_rem")
        pair_mid = sem("pair_mid")
        pair_low = sem("pair_low")
        pairs_summed = sem("pairs_summed")
        pairs_evacuated = sem("pairs_evacuated")
        transformed = sem("transformed")
        tile_added = sem("tile_added")
        turns_added = sem("turns_added")
        s_weight = sem("s_weight")
        s_rows = sem("s_rows")
        s_cols = sem("s_cols")
        s_resw = sem("s_resw")
        bases_found = sem("bases_found")
        bases_stored = sem("bases_stored")
        bases_loaded = sem("bases_loaded")
        flag_ready = sem("flag_ready")
        w_product = sem("w_product")
        w_copied = sem("w_copied")
        w_parts = sem("w_parts")
        x_parts = sem("x_parts")
        x_step = sem("x_step")
        unit_full = sem("unit_full")
        act_free = sem("act_free")
        dve_free = sem("dve_free")
        dve_step = sem("dve_step")
        stored = [sem(f"stored_{s}") for s in range(2 * UNITS)]
        edges_used = sem("edges_used")
        h_zeroed = sem("h_zeroed")
        keys_made = sem("keys_made")
        key_unshifted = sem("key_unshifted")
        iota_step = sem("iota_step")
        constants = sem("constants")
        index_ready = sem("index_ready")
        gathered = [sem(f"gathered_{s}") for s in range(SLOTS)]
        select_ready = sem("select_ready")
        window_summed = sem("window_summed")
        sum_free = sem("sum_free")
        h_done = sem("h_done")
        res_product = sem("res_product")
        res_ready = sem("res_ready")
        relu_ready = sem("relu_ready")
        y_ready = sem("y_ready")
        stats_ready = sem("stats_ready")
        bn_step = sem("bn_step")
        shift_product = sem("shift_product")
        shift_step = sem("shift_step")
        z_product = sem("z_product")
        z_shifted = sem("z_shifted")
        z_squared = sem("z_squared")
        var_ready = sem("var_ready")
        std_ready = sem("std_ready")
        inverse_ready = sem("inverse_ready")
        z_ready = sem("z_ready")
        z_stored = [sem(f"z_stored_{s}") for s in range(ZS)]

        block = ctx.enter_context(nc.Block())

        def unit_psum(u):
            return psum[:, u * UNIT:(u + 1) * UNIT]

        def stage(t, u):
            s = (t % 2) * UNITS + u
            return y_stage[:, s * UNIT:(s + 1) * UNIT]

        def wait(engine, semaphore, value):
            if not isinstance(value, int) or value > 0:
                engine.wait_ge(semaphore, value)

        def modes(engine):
            engine.wait_ge(flag_ready, 1)
            group_span = engine.value_load(span_max[0:1, 0:1], min_val=0, max_val=N_NODES)
            direct_span = engine.value_load(span_max[0:1, 1:2], min_val=0, max_val=2 * N_NODES)
            return group_span, direct_span

        def table_stored(engine):
            for s in range(2 * UNITS):
                engine.wait_ge(stored[s], 16 * (NODE_TILES // 2))

        @block.sync
        def _(sp):
            sp.dma_start(basis_sb, basis2).then_inc(s_basis, 16)
            sp.dma_start(xT[:, 0:2 * P], x2T[:, 0:2 * P]).then_inc(s_x, 16)
            sp.dma_start(dst_rows, dst_flat[0:GP * GJ * GE].rearrange("(p n) -> p n", p=GP)).then_inc(s_rows, 16)
            sp.dma_start(dst_last, dst_flat[GP * GJ * GE:N_EDGES].unsqueeze(0)).then_inc(s_rows, 16)
            sp.dma_start(dst_direct, dst_flat[0:DIRECT_TILES * P].rearrange("(p n) -> p n", p=TURNS)).then_inc(s_rows, 16)
            sp.dma_start(xT[:, 2 * P:NODES_PADDED], x2T[:, 2 * P:NODES_PADDED]).then_inc(s_x_rest, 16)
            sp.wait_ge(bases_found, 1)
            sp.dma_start(base_dram[0:GP * GJ].rearrange("(p n) -> p n", p=GP), base_g[:, :]).then_inc(bases_stored, 16)
            sp.dma_start(span_dram[0:GP * GJ].rearrange("(p n) -> p n", p=GP), span_g[:, :]).then_inc(bases_stored, 16)
            sp.dma_start(base_dram[GP * GJ:GROUPS].unsqueeze(0), last_bs[:, 0:1]).then_inc(bases_stored, 16)
            sp.dma_start(span_dram[GP * GJ:GROUPS].unsqueeze(0), last_bs[:, 1:2]).then_inc(bases_stored, 16)
            sp.dma_start(direct_base_dram.rearrange("(p n) -> p n", p=TURNS), base_d[:, :]).then_inc(bases_stored, 16)
            sp.dma_start(direct_span_dram.rearrange("(p n) -> p n", p=TURNS), span_d[:, :]).then_inc(bases_stored, 16)
            sp.wait_ge(bases_stored, 96)
            sp.dma_start(base_row[:, :], base_dram.partition_broadcast(P)).then_inc(bases_loaded, 16)
            sp.dma_start(span_row[:, :], span_dram.unsqueeze(0)).then_inc(bases_loaded, 16)
            sp.dma_start(direct_base_row[:, :], direct_base_dram.partition_broadcast(P)).then_inc(bases_loaded, 16)
            sp.dma_start(direct_span_row[:, :], direct_span_dram.unsqueeze(0)).then_inc(bases_loaded, 16)
            with sp.Fori(0, NODE_TILES // 2) as i:
                for t in range(2):
                    for u in range(UNITS):
                        sp.wait_ge(act_free if u % 2 == 0 else dve_free, 4 * i + 2 * t + u // 2 + 3)
                        sp.dma_start(table_tiles[2 * i + t, :, u * UNIT:(u + 1) * UNIT],
                                     stage(t, u)).then_inc(stored[t * UNITS + u], 16)
            table_stored(sp)
            for s in range(RING):
                sp.wait_ge(direct_stored[s], 16 * len(range(s, TURNS, RING)))
            group_span, direct_span = modes(sp)
            with sp.If((group_span < WINDOW) & (direct_span < NARROW)):
                def load_direct(i):
                    for q in range(QUADS):
                        wait(sp, pair_scaled, QUADS * (i - 1) + q + 1)
                        sp.dma_start(direct_x[:, q, :], x_direct[i, :, q * PAIR * F:(q + 1) * PAIR * F]
                                     ).then_inc(direct_loaded[q], 16)

                load_direct(0)
                with sp.Fori(1, TURNS) as i:
                    load_direct(i)
            for b, (n0, m, k) in enumerate(BLOCKS):
                sp.wait_ge(z_ready, b + 1)
                sp.dma_start(out[n0:n0 + m * k, :].rearrange("(p k) f -> p (k f)", k=k),
                             z_buf[0:m, b % ZS, 0:k * F]).then_inc(z_stored[b % ZS], 16)
            for s in range(ZS):
                sp.wait_ge(z_stored[s], 16 * len(range(s, len(BLOCKS), ZS)))

        @block.gpsimd
        def _(pool):
            nc.gpsimd.iota(node_iota[:, :], [[1, WIDE]], base=0, channel_multiplier=0,
                           allow_small_or_imprecise_dtypes=True).then_inc(constants, 1)
            nc.gpsimd.iota(key_iota[:, :], [[1, 2], [RELS, NARROW], [2, REL_PAIRS]], base=0, channel_multiplier=0,
                           allow_small_or_imprecise_dtypes=True).then_inc(constants, 1)
            nc.gpsimd.memset(combine[:, :], 0.0).then_inc(constants, 1)
            nc.gpsimd.memset(identity[:, :], 0.0).then_inc(constants, 1)
            nc.gpsimd.memset(ones[:, :], 1.0).then_inc(constants, 1)
            nc.gpsimd.memset(eps_col[:, :], BN_EPS).then_inc(constants, 1)
            pool.wait_ge(constants, 7)
            nc.gpsimd.affine_select(out=identity[:, :], in_=identity[:, :], compare_op=ALU.not_equal, fill=1.0,
                                    base=0, pattern=[[-1, F]], channel_multiplier=1).then_inc(constants, 1)
            nc.gpsimd.affine_select(out=combine[:, :], in_=combine[:, :], compare_op=ALU.not_equal, fill=1.0,
                                    base=-F, pattern=[[-1, F]], channel_multiplier=1).then_inc(constants, 1)
            pool.wait_ge(s_direct_src, 16)

            def gather_direct(b, s, lap):
                wait(pool, direct_stored[s], 16 * lap)
                nc.gpsimd.tensor_copy(direct_index[:, s, :],
                                      direct_src[:, bass.ds(b * DIRECT_PER_TURN, DIRECT_PER_TURN)]
                                      ).then_inc(direct_copied, 1)
                pool.wait_ge(direct_copied, b + 1)
                pool.sem_inc(wait_carrier, 1)
                for k in range(DIRECT_PER_TURN):
                    pool.indirect_dma_start(
                        out=direct_rows[:, s, k, :], out_offset=None, in_=x_rows,
                        in_offset=bass.IndirectOffsetOnAxis(ap=direct_index[:, s, k:k + 1], axis=0),
                    ).then_inc(direct_gathered[s * DIRECT_PER_TURN + k], 16)

            def store_direct(b, s, lap):
                for k in range(DIRECT_PER_TURN):
                    pool.wait_ge(direct_gathered[s * DIRECT_PER_TURN + k], 16 * (lap + 1))
                pool.sem_inc(wait_carrier, 1)
                pool.dma_start(x_direct[b, :, :], direct_rows[:, s, :, :].rearrange("p k f -> p (k f)")
                               ).then_inc(direct_stored[s], 16)

            pool.wait_ge(w_parts, UNITS)
            for b in range(RING):
                gather_direct(b, b, 0)
                if b >= BEHIND:
                    store_direct(b - BEHIND, b - BEHIND, 0)
            with pool.Fori(1, TURNS // RING) as lap:
                for s in range(RING):
                    gather_direct(RING * lap + s, s, lap)
                    store_direct(RING * lap + s - BEHIND, (s - BEHIND) % RING, lap if s >= BEHIND else lap - 1)
            for b in range(TURNS // RING * RING, TURNS + BEHIND):
                if b < TURNS:
                    gather_direct(b, b % RING, b // RING)
                store_direct(b - BEHIND, (b - BEHIND) % RING, (b - BEHIND) // RING)
            pool.wait_ge(flag_ready, 1)
            for s in range(RING):
                pool.wait_ge(direct_stored[s], 16 * len(range(s, TURNS, RING)))
            nc.gpsimd.memset(hT, 0.0).then_inc(h_zeroed, 1)
            for s in range(2 * UNITS):
                pool.wait_ge(stored[s], 16 * (NODE_TILES // 2))

            def gather(slot, rows=P):
                pool.indirect_dma_start(
                    out=gathered_rows[0:rows, slot, :], out_offset=None, in_=table,
                    in_offset=bass.IndirectOffsetOnAxis(ap=index_slot[0:rows, slot:slot + 1], axis=0),
                ).then_inc(gathered[slot], 16)

            def gather_groups(first, turns):
                with pool.Fori(0, turns) as i:
                    for q in range(QUADS):
                        pool.wait_ge(index_ready, QUADS * i + q + 1)
                        pool.sem_inc(wait_carrier, 1)
                        for k in range(GROUP):
                            gather(q * GROUP + k)
                for n in range(turns * QUADS, GROUPS - first):
                    pool.wait_ge(index_ready, n + 1)
                    for k in range(GROUP):
                        tile = (first + n) * GROUP + k
                        if tile < EDGE_TILES:
                            gather(n % QUADS * GROUP + k, P if tile < EDGE_TILES - 1 else LAST_TILE_ROWS)

            group_span, direct_span = modes(pool)
            with pool.If((group_span < WINDOW) & (direct_span < NARROW)):
                gather_groups(FIRST_GROUP, TURNS)
            with pool.Else():
                gather_groups(0, ALL_TURNS)

        @block.tensor
        def _(pe):
            pe.wait_ge(s_basis, 16)
            pe.wait_ge(s_comp, 16)
            for o in range(F):
                last = nc.tensor.matmul(psum[:, o * RELS:(o + 1) * RELS], basis_sb[:, o, :], comp_sb[:, :],
                                        start=True, stop=True)
            last.then_inc(w_product, 1)
            pe.wait_ge(w_copied, 2)
            with pe.Fori(0, NODE_TILES // 2) as i:
                for t in range(2):
                    pe.wait_ge(x_parts, 2 * i + t + 1)
                    for u in range(UNITS):
                        pe.wait_ge(w_parts, u + 1)
                        pe.wait_ge(act_free if u % 2 == 0 else dve_free, 4 * i + 2 * t + u // 2 + 1)
                        for c in range(2 * u, 2 * u + 2):
                            at = slice(c * BANK, (c + 1) * BANK)
                            nc.tensor.matmul(psum[:, at], x_hl[:, t, :], w_lowhigh[:, at], start=True, stop=False)
                            nc.tensor.matmul(psum[:, at], x_hm[:, t, :], w_mid[:, at], start=False, stop=False)
                            last = nc.tensor.matmul(psum[:, at], x_hm[:, t, :], w_high[:, at], start=False, stop=True)
                        last.then_inc(unit_full, 1)
            pe.wait_ge(act_free, 2 * NODE_TILES + 2)
            pe.wait_ge(dve_free, 2 * NODE_TILES + 2)

            def sum_group(q, turn, rhs, width, ready, free, tiles=GROUP, last_rows=P):
                pe.wait_ge(select_ready, ready)
                pe.wait_ge(sum_free, free)
                for k in range(tiles):
                    slot = q * GROUP + k
                    rows = last_rows if k == tiles - 1 else P
                    pe.wait_ge(gathered[slot], 16 * (turn + 1))
                    last = nc.tensor.matmul(psum[0:F, q * BANK:q * BANK + width], gathered_rows[0:rows, slot, :],
                                            rhs(k, rows), start=(k == 0), stop=(k == tiles - 1))
                last.then_inc(window_summed, 1)

            def tail(g):
                tiles = min(GROUP, EDGE_TILES - g * GROUP)
                return dict(tiles=tiles, last_rows=LAST_TILE_ROWS if g == GROUPS - 1 else P)

            def narrow(q):
                return lambda k, rows: select[0:rows, q % 2, k, :]

            def wide(k, rows):
                return wide_select[0:rows, k, :]

            def sum_pair(n, q):
                pe.wait_ge(pair_selected, n + 1)
                pe.wait_ge(pair_low, n + 1)
                wait(pe, pairs_evacuated, n - 1)
                bank = (QUADS + q % 2) * BANK
                half = KEYS // 2
                for j in range(PAIR):
                    for part in range(3):
                        for parity in range(2):
                            last = nc.tensor.matmul(
                                psum[parity * F:(parity + 1) * F, bank + j * half:bank + (j + 1) * half],
                                parts[:, part, q % 2, j * F:(j + 1) * F],
                                pair_select[:, q % 2, j, parity * half:(parity + 1) * half],
                                start=(part == 0), stop=(part == 2))
                last.then_inc(pairs_summed, 1)

            def transform(i, half):
                if half == 0:
                    pe.wait_ge(pairs_evacuated, QUADS * (i + 1))
                    pe.wait_ge(turns_added, i + 1)
                for r in range(half * REL_PAIRS // 2, (half + 1) * REL_PAIRS // 2):
                    last = nc.tensor.matmul(psum[0:F, 6 * BANK:6 * BANK + DIRECT_PER_TURN * NARROW], w_pairs[:, r, :],
                                            pair_sums[:, r, :], start=(r == 0), stop=(r == REL_PAIRS - 1))
                if half == 1:
                    last.then_inc(transformed, 1)

            group_span, direct_span = modes(pe)
            with pe.If((group_span < WINDOW) & (direct_span < NARROW)):
                def both(i):
                    for q in range(QUADS):
                        n = QUADS * i + q
                        sum_group(q, i, narrow(q), WINDOW, n + 1, n + 1)
                        if q < 2 and not (isinstance(i, int) and i == 0):
                            transform(i - 1, q)
                        sum_pair(n, q)

                both(0)
                with pe.Fori(1, TURNS) as i:
                    both(i)
                for n in range(TURNS * QUADS, GROUPS - FIRST_GROUP):
                    sum_group(n % QUADS, n // QUADS, narrow(n % QUADS), WINDOW, n + 1, n + 1, **tail(FIRST_GROUP + n))
                transform(TURNS - 1, 0)
                transform(TURNS - 1, 1)
            with pe.Else():
                with pe.If(group_span < WINDOW):
                    with pe.Fori(0, ALL_TURNS) as i:
                        for q in range(QUADS):
                            n = QUADS * i + q + 1
                            sum_group(q, i, narrow(q), WINDOW, n, n)
                    for g in range(ALL_TURNS * QUADS, GROUPS):
                        sum_group(g % QUADS, g // QUADS, narrow(g % QUADS), WINDOW, g + 1, g + 1, **tail(g))
                with pe.Else():
                    with pe.Fori(0, ALL_TURNS) as i:
                        for q in range(QUADS):
                            with pe.Fori(0, WIDE_WINDOWS) as w:
                                n = (QUADS * i + q) * WIDE_WINDOWS + w + 1
                                sum_group(q, i, wide, WIDE, n, n + QUADS - 1)
                    for g in range(ALL_TURNS * QUADS, GROUPS):
                        with pe.Fori(0, WIDE_WINDOWS) as w:
                            n = g * WIDE_WINDOWS + w + 1
                            sum_group(g % QUADS, g // QUADS, wide, WIDE, n, n + QUADS - 1, **tail(g))
                pe.sem_inc(wait_carrier, 1)
            pe.wait_ge(h_done, 1)
            pe.wait_ge(s_resw, 16)
            pe.wait_ge(constants, 9)
            for c, (c0, m) in enumerate(CHUNKS):
                if c >= 2:
                    pe.wait_ge(res_ready, c - 1)
                nc.tensor.matmul(psum[0:F, (4 + c % 2) * BANK:(4 + c % 2) * BANK + m], res_w[:, :], xT[:, c0:c0 + m],
                                 start=True, stop=True).then_inc(res_product, 1)
            pe.wait_ge(bn_step, BN_STEPS)
            nc.tensor.matmul(psum[:, 0:F], ones[:, :], shift_diag[:, :], start=True, stop=True).then_inc(shift_product, 1)
            pe.wait_ge(res_ready, len(CHUNKS))
            for b, (n0, m, k) in enumerate(BLOCKS):
                if b >= 2:
                    pe.wait_ge(z_shifted, b - 1)
                for j in range(k):
                    at = (4 + b % 2) * BANK + j * F
                    last = nc.tensor.matmul(psum[0:m, at:at + F], xT[:, n0 + j:n0 + j + (m - 1) * k + 1:k],
                                            combine[:, :], start=True, stop=True)
                last.then_inc(z_product, 1)

        @block.scalar
        def _(act):
            act.dma_start(comp_sb[:, :], compT).then_inc(s_comp, 16)
            act.dma_start(direct_src[:, :], src_cols[:, 0:DIRECT_TILES]).then_inc(s_direct_src, 16)
            act.dma_start(row_index[:, :], src_cols).then_inc(s_edges, 16)
            act.dma_start(type_i, type_cols).then_inc(s_edges, 16)
            act.dma_start(dst_i, dst_cols).then_inc(s_edges, 16)
            act.dma_start(weight[:, :], weight_cols).then_inc(s_weight, 16)
            act.dma_start(cols[:, 0:1], bias_col).then_inc(s_cols, 16)
            act.dma_start(cols[:, 1:2], res_b_col).then_inc(s_cols, 16)
            act.dma_start(cols[:, 2:3], gamma_col).then_inc(s_cols, 16)
            act.dma_start(cols[:, 3:4], beta_col).then_inc(s_cols, 16)
            act.dma_start(res_w[0:F, :], res_wT).then_inc(s_resw, 16)
            act.wait_ge(w_product, 1)
            w_out = w_f32.rearrange("p (r o) -> p o r", o=F)
            w_in = psum[:, :].rearrange("p (o r) -> p o r", r=RELS)
            nc.scalar.copy(w_out[:, 0:F // 2, :], w_in[:, 0:F // 2, :]).then_inc(w_copied, 1)
            act.wait_ge(w_copied, 2)
            w_even_odd = w_f32.rearrange("p (r t o) -> p r t o", t=2, o=F)
            nc.scalar.copy(w_pairs[0:F, :, :], w_even_odd[0:F, :, 0, :]).then_inc(w_copied, 1)
            nc.scalar.copy(w_pairs[F:P, :, :], w_even_odd[F:P, :, 1, :]).then_inc(w_copied, 1)
            act.sem_inc(act_free, 2)
            act.wait_ge(edges_used, 1)
            for peeled in (True, False):
                def evacuate(i):
                    for t in range(2):
                        for u in range(0, UNITS, 2):
                            act.wait_ge(unit_full, UNITS * (2 * i + t) + u + 1)
                            if not peeled:
                                act.wait_ge(stored[t * UNITS + u], 16 * i)
                            nc.scalar.copy(stage(t, u), unit_psum(u)).then_inc(act_free, 1)
                if peeled:
                    evacuate(0)
                else:
                    with act.Fori(1, NODE_TILES // 2) as i:
                        evacuate(i)
            group_span, direct_span = modes(act)
            with act.If((group_span < WINDOW) & (direct_span < NARROW)):
                def split_pair(n, q):
                    act.wait_ge(pair_scaled, n + 1)
                    wait(act, pairs_summed, n - 1)
                    nc.scalar.copy(parts[:, 0, q % 2, :], scaled[:, q % 2, :]).then_inc(pair_high, 1)
                    act.wait_ge(pair_rem, n + 1)
                    nc.scalar.copy(parts[:, 1, q % 2, :], scaled_rem[:, q % 2, :]).then_inc(pair_mid, 1)

                def evacuate_pair(n, i, q):
                    act.wait_ge(pairs_summed, n + 1)
                    if q == 0:
                        wait(act, transformed, i)
                    bank = (QUADS + q % 2) * BANK
                    columns = PAIR * NARROW
                    nc.scalar.copy(
                        pair_sums[:, :, q * columns:(q + 1) * columns].rearrange("p r (j n) -> p j n r", j=PAIR),
                        psum[:, bank:bank + BANK].rearrange("p (j n r) -> p j n r", j=PAIR, n=NARROW),
                    ).then_inc(pairs_evacuated, 1)

                def pairs(i):
                    for q in range(QUADS):
                        n = QUADS * i + q
                        split_pair(n, q)
                        if q > 0:
                            evacuate_pair(n - 1, i, q - 1)
                        elif not (isinstance(i, int) and i == 0):
                            evacuate_pair(n - 1, i - 1, QUADS - 1)

                pairs(0)
                with act.Fori(1, TURNS) as i:
                    pairs(i)
                evacuate_pair(TURNS * QUADS - 1, TURNS - 1, QUADS - 1)
            act.wait_ge(s_cols, 64)
            act.wait_ge(h_done, 1)
            for c, (c0, m) in enumerate(CHUNKS):
                nc.scalar.activation(hT[:, c0:c0 + m], hT[:, c0:c0 + m], ACT.Relu,
                                     bias=cols[:, 0:1]).then_inc(relu_ready, 1)
                act.wait_ge(res_product, c + 1)
                if c >= 2:
                    act.wait_ge(y_ready, c - 1)
                nc.scalar.activation(res_y[:, c % 2, 0:m], psum[0:F, (4 + c % 2) * BANK:(4 + c % 2) * BANK + m],
                                     ACT.Relu, bias=cols[:, 1:2]).then_inc(res_ready, 1)
            act.wait_ge(bn_step, 1)
            nc.scalar.activation(affine[:, 0:1], mv[:, 1:2], ACT.Sqrt, bias=eps_col[0:F, :]).then_inc(bn_step, 1)
            for b in range(len(BLOCKS) + 1):
                if b < len(BLOCKS):
                    _, m, k = BLOCKS[b]
                    act.wait_ge(z_shifted, b + 1)
                    if b >= 2:
                        act.wait_ge(var_ready, b - 1)
                    nc.scalar.activation(squares[0:m, b % 2, 0:k * F], z_buf[0:m, b % ZS, 0:k * F],
                                         ACT.Square).then_inc(z_squared, 1)
                if b >= 1:
                    _, m, k = BLOCKS[b - 1]
                    act.wait_ge(var_ready, b)
                    sums = deviation[0:m, (b - 1) % ZS, 0, 0:k]
                    nc.scalar.activation(sums, sums, ACT.Sqrt, bias=eps_col[0:m, :],
                                         scale=1.0 / F).then_inc(std_ready, 1)

        @block.vector
        def _(dve):
            steps = [0]

            def step(instruction):
                steps[0] += 1
                instruction.then_inc(dve_step, 1)
                dve.wait_ge(dve_step, steps[0])

            nc.vector.memset(res_w[F:P, :], 0.0).then_inc(constants, 1)
            dve.wait_ge(s_rows, 48)
            grouped = dst_rows.rearrange("p (g e) -> p g e", g=GJ)
            direct = dst_direct.rearrange("p (t e) -> p t e", t=DIRECT_PER_TURN)
            for least, most, targets in ((base_g[:, :], span_g[:, :], grouped), (base_d[:, :], span_d[:, :], direct),
                                         (last_bs[:, 0:1], last_bs[:, 1:2], dst_last)):
                nc.vector.tensor_reduce(least, targets, AX.X, ALU.min).then_inc(dve_step, 1)
                nc.vector.tensor_reduce(most, targets, AX.X, ALU.max).then_inc(dve_step, 1)
            steps[0] = 6
            dve.wait_ge(dve_step, 6)
            step(nc.vector.tensor_tensor(span_g[:, :], span_g[:, :], base_g[:, :], ALU.subtract))
            step(nc.vector.tensor_tensor(span_d[:, :], span_d[:, :], base_d[:, :], ALU.subtract))
            nc.vector.tensor_tensor(last_bs[:, 1:2], last_bs[:, 1:2], last_bs[:, 0:1], ALU.subtract).then_inc(bases_found, 1)
            dve.wait_ge(w_product, 1)
            w_out = w_f32.rearrange("p (r o) -> p o r", o=F)
            w_in = psum[:, :].rearrange("p (o r) -> p o r", r=RELS)
            nc.vector.tensor_copy(w_out[:, F // 2:F, :], w_in[:, F // 2:F, :]).then_inc(w_copied, 1)
            dve.wait_ge(w_copied, 2)
            dve.sem_inc(dve_free, 2)

            def split_w(u):
                at = slice(u * UNIT, (u + 1) * UNIT)
                step(nc.vector.tensor_copy(w_high[:, at], w_f32[:, at]))
                nc.vector.tensor_copy(w_lowhigh[F:P, at], w_high[F:P, at]).then_inc(dve_step, 1)
                steps[0] += 1
                step(nc.vector.tensor_tensor(w_rem, w_f32[:, at], w_high[:, at], ALU.subtract))
                step(nc.vector.tensor_copy(w_mid[:, at], w_rem))
                nc.vector.tensor_tensor(w_lowhigh[0:F, at], w_rem[0:F, :], w_mid[0:F, at],
                                        ALU.subtract).then_inc(w_parts, 1)
                dve.wait_ge(w_parts, u + 1)

            def split_x(tile, t):
                wait(dve, unit_full, UNITS * (tile - 1))
                x_tile = bass.ds(tile * P, P)
                nc.vector.tensor_copy(x_hm[:, t, :], xT[:, x_tile]).then_inc(x_step, 1)
                nc.vector.tensor_copy(x_hl[:, t, :], xT[:, x_tile]).then_inc(x_step, 1)
                dve.wait_ge(x_step, 4 * tile + 2)
                nc.vector.tensor_tensor(x_rem[F:P, t, :], xT[F:P, x_tile], x_hl[F:P, t, :],
                                        ALU.subtract).then_inc(x_step, 1)
                dve.wait_ge(x_step, 4 * tile + 3)
                nc.vector.tensor_copy(x_hm[F:P, t, :], x_rem[F:P, t, :]).then_inc(x_step, 1)
                dve.wait_ge(x_step, 4 * tile + 4)
                nc.vector.tensor_tensor(x_hl[F:P, t, :], x_rem[F:P, t, :], x_hm[F:P, t, :],
                                        ALU.subtract).then_inc(x_parts, 1)

            split_w(0)
            dve.wait_ge(s_x, 16)
            split_x(0, 0)
            for u in range(1, UNITS):
                split_w(u)
            dve.wait_ge(s_edges, 48)
            step(nc.vector.scalar_tensor_tensor(out=row_index[:, :], in0=row_index[:, :], scalar=float(RELS),
                                                in1=type_i, op0=ALU.mult, op1=ALU.add))
            step(nc.vector.tensor_copy(dst_key[:, :], dst_i))
            step(nc.vector.tensor_copy(direct_key[:, :], type_i[:, 0:DIRECT_TILES]))
            dve.sem_inc(edges_used, 1)

            def table_turn(i, first=False, last=False):
                for t in range(2):
                    tile = 2 * i + t
                    if not (last and t == 1):
                        split_x(tile + 1, (t + 1) % 2)
                    for u in range(1, UNITS, 2):
                        dve.wait_ge(unit_full, UNITS * tile + u + 1)
                        if not first:
                            dve.wait_ge(stored[t * UNITS + u], 16 * i)
                        nc.vector.tensor_copy(stage(t, u), unit_psum(u)).then_inc(dve_free, 1)

            dve.wait_ge(s_x_rest, 16)
            table_turn(0, first=True)
            dve.wait_ge(bases_loaded, 64)
            nc.vector.tensor_tensor(relative[:, :], dst_key[:, 0:DIRECT_TILES], direct_base_row[:, :],
                                    ALU.subtract).then_inc(keys_made, 1)
            dve.wait_ge(keys_made, 1)
            nc.vector.scalar_tensor_tensor(out=direct_key[:, :], in0=relative[:, :], scalar=float(RELS),
                                           in1=direct_key[:, :], op0=ALU.mult, op1=ALU.add).then_inc(keys_made, 1)
            whole = dst_key[:, 0:GROUPS * GROUP].rearrange("p (g k) -> p g k", k=GROUP)
            bases = base_row[:, :].unsqueeze(2).broadcast_to([P, GROUPS, GROUP])
            nc.vector.tensor_tensor(whole, whole, bases, ALU.subtract).then_inc(keys_made, 1)
            nc.vector.tensor_reduce(span_max[:, 0:1], span_row[:, :], AX.X, ALU.max).then_inc(keys_made, 1)
            nc.vector.tensor_reduce(span_max[:, 1:2], direct_span_row[:, :], AX.X, ALU.max).then_inc(keys_made, 1)
            dve.wait_ge(keys_made, 5)
            dve.sem_inc(flag_ready, 1)
            with dve.Fori(1, NODE_TILES // 2 - 1) as i:
                table_turn(i)
            table_turn(NODE_TILES // 2 - 1, last=True)
            table_stored(dve)

            def indices(g, q):
                slots = slice(q * GROUP, (q + 1) * GROUP)
                nc.vector.tensor_copy(index_slot[:, slots], row_index[:, bass.ds(g * GROUP, GROUP)]
                                      ).then_inc(index_ready, 1)

            dve.sem_inc(sum_free, QUADS)
            dve.wait_ge(constants, 9)
            dve.wait_ge(s_weight, 16)
            group_span, direct_span = modes(dve)

            def selection(g, s):
                for k in range(GROUP):
                    t = g * GROUP + k
                    last = nc.vector.tensor_scalar(select[:, s, k, :], node_iota[:, 0:WINDOW],
                                                   dst_key[:, bass.ds(t, 1)], weight[:, bass.ds(t, 1)],
                                                   ALU.is_equal, ALU.mult)
                last.then_inc(select_ready, 1)

            def load_bases(row, first, count):
                return nc.values_load_multi_w_load_instructions(
                    row[0:1, bass.ds(first, count)], engines=[mybir.EngineType.DVE], min_val=0, max_val=N_NODES - 1,
                    skip_runtime_bounds_check_because="targets are node numbers")[1]

            def add_window(n, q, base):
                window = hT[:, bass.ds(base, WINDOW)]
                dve.wait_ge(sum_free, n + QUADS)
                nc.vector.tensor_tensor(window, window, psum[0:F, q * BANK:q * BANK + WINDOW],
                                        ALU.add).then_inc(sum_free, 1)

            def prepare_pair(n, i, q):
                t = n * PAIR
                dve.wait_ge(direct_loaded[q], 16 * (i + 1))
                nc.vector.tensor_tensor(scaled[:, q % 2, :].rearrange("p (j f) -> p j f", j=PAIR),
                                        direct_x[:, q, :].rearrange("p (j f) -> p j f", j=PAIR),
                                        weight[:, bass.ds(t, PAIR)].unsqueeze(2).broadcast_to([P, PAIR, F]),
                                        ALU.mult).then_inc(pair_scaled, 1)
                wait(dve, pairs_summed, n - 1)

            def select_pair(n, q, j):
                last = nc.vector.tensor_scalar(pair_select[:, q % 2, j, :], key_iota[:, :],
                                               direct_key[:, bass.ds(n * PAIR + j, 1)], None, ALU.is_equal)
                if j == PAIR - 1:
                    last.then_inc(pair_selected, 1)

            def remainder(n, q):
                dve.wait_ge(pair_high, n + 1)
                nc.vector.tensor_tensor(scaled_rem[:, q % 2, :], scaled[:, q % 2, :], parts[:, 0, q % 2, :],
                                        ALU.subtract).then_inc(pair_rem, 1)

            def finish_pair(n, q):
                dve.wait_ge(pair_mid, n + 1)
                nc.vector.tensor_tensor(parts[:, 2, q % 2, :], scaled_rem[:, q % 2, :], parts[:, 1, q % 2, :],
                                        ALU.subtract).then_inc(pair_low, 1)

            def add_direct(i, j, base):
                if j == 0:
                    dve.wait_ge(transformed, i + 1)
                else:
                    dve.wait_ge(tile_added, i * DIRECT_PER_TURN + j)
                window = hT[:, bass.ds(base, NARROW)]
                at = 6 * BANK + j * NARROW
                nc.vector.tensor_tensor(window, window, psum[0:F, at:at + NARROW], ALU.add).then_inc(tile_added, 1)
                if j == DIRECT_PER_TURN - 1:
                    dve.wait_ge(tile_added, (i + 1) * DIRECT_PER_TURN)
                    dve.sem_inc(turns_added, 1)

            def narrow_tail(first, turns):
                for n in range(turns * QUADS, GROUPS - first):
                    g = first + n
                    if g + 1 < GROUPS:
                        selection(g + 1, (n + 1) % 2)
                    dve.wait_ge(window_summed, n + 1)
                    add_window(n, n % QUADS, load_bases(base_row, g, 1)[0])
                dve.wait_ge(sum_free, GROUPS - first + QUADS)

            with dve.If((group_span < WINDOW) & (direct_span < NARROW)):
                for q in range(QUADS):
                    indices(FIRST_GROUP + q, q)
                dve.wait_ge(h_zeroed, 1)
                dve.sem_inc(turns_added, 1)
                selection(FIRST_GROUP, 0)

                def both(i):
                    first = isinstance(i, int) and i == 0
                    for q in range(QUADS):
                        n = QUADS * i + q
                        g = FIRST_GROUP + n
                        adds = q >= 2 and not first

                        def add(k):
                            if adds:
                                j = (q - 2) * 4 + k
                                add_direct(i - 1, j, direct_bases[j])

                        prepare_pair(n, i, q)
                        if adds:
                            dve.wait_ge(sum_free, n + QUADS)
                        add(0)
                        select_pair(n, q, 0)
                        add(1)
                        select_pair(n, q, 1)
                        add(2)
                        remainder(n, q)
                        selection(g + 1, (q + 1) % 2)
                        if q == 0:
                            starts = load_bases(base_row, FIRST_GROUP + QUADS * i, QUADS)
                        if q == 1 and not first:
                            direct_bases = load_bases(direct_base_row, (i - 1) * DIRECT_PER_TURN, DIRECT_PER_TURN)
                        add(3)
                        finish_pair(n, q)
                        dve.wait_ge(window_summed, n + 1)
                        indices(g + QUADS, q)
                        if adds:
                            dve.wait_ge(tile_added, (i - 1) * DIRECT_PER_TURN + (q - 1) * 4)
                        add_window(n, q, starts[q])

                both(0)
                with dve.Fori(1, TURNS) as i:
                    both(i)
                narrow_tail(FIRST_GROUP, TURNS)
                last_bases = load_bases(direct_base_row, (TURNS - 1) * DIRECT_PER_TURN, DIRECT_PER_TURN)
                dve.wait_ge(sum_free, GROUPS - FIRST_GROUP + QUADS)
                for j in range(DIRECT_PER_TURN):
                    add_direct(TURNS - 1, j, last_bases[j])
            with dve.Else():
                for q in range(QUADS):
                    indices(q, q)
                dve.wait_ge(h_zeroed, 1)
                with dve.If(group_span < WINDOW):
                    selection(0, 0)
                    with dve.Fori(0, ALL_TURNS) as i:
                        starts = load_bases(base_row, QUADS * i, QUADS)
                        for q in range(QUADS):
                            g = QUADS * i + q
                            selection(g + 1, (q + 1) % 2)
                            dve.wait_ge(window_summed, g + 1)
                            indices(g + QUADS, q)
                            add_window(g, q, starts[q])
                    narrow_tail(0, ALL_TURNS)
                with dve.Else():
                    nc.vector.tensor_tensor(whole, whole, bases, ALU.add).then_inc(key_unshifted, 1)
                    dve.wait_ge(key_unshifted, 1)

                    def add_wide(g, q, w):
                        n = g * WIDE_WINDOWS + w
                        for k in range(GROUP):
                            t = g * GROUP + k
                            last = nc.vector.tensor_scalar(wide_select[:, k, :], wide_iota[:, :],
                                                           dst_key[:, bass.ds(t, 1)], weight[:, bass.ds(t, 1)],
                                                           ALU.is_equal, ALU.mult)
                        last.then_inc(select_ready, 1)
                        dve.wait_ge(window_summed, n + 1)
                        window = hT[:, bass.ds(w * WIDE, WIDE)]
                        nc.vector.tensor_tensor(window, window, psum[0:F, q * BANK:(q + 1) * BANK],
                                                ALU.add).then_inc(sum_free, 1)
                        dve.wait_ge(sum_free, n + 1 + QUADS)
                        nc.vector.tensor_scalar(wide_iota[:, :], wide_iota[:, :], float(WIDE), None,
                                                ALU.add).then_inc(iota_step, 1)
                        dve.wait_ge(iota_step, n + g + 2)

                    def group(g, q):
                        nc.vector.tensor_copy(wide_iota[:, :], node_iota[:, :]).then_inc(iota_step, 1)
                        dve.wait_ge(iota_step, g * (WIDE_WINDOWS + 1) + 1)
                        dve.sem_inc(wait_carrier, 1)
                        with dve.Fori(0, WIDE_WINDOWS) as w:
                            add_wide(g, q, w)

                    with dve.Fori(0, ALL_TURNS) as i:
                        for q in range(QUADS):
                            group(QUADS * i + q, q)
                            indices(QUADS * i + q + QUADS, q)
                    for g in range(ALL_TURNS * QUADS, GROUPS):
                        group(g, g % QUADS)
                dve.sem_inc(wait_carrier, 1)
            dve.sem_inc(h_done, 1)

            for c, (c0, m) in enumerate(CHUNKS):
                dve.wait_ge(relu_ready, c + 1)
                dve.wait_ge(res_ready, c + 1)
                nc.vector.tensor_tensor(xT[0:F, c0:c0 + m], hT[:, c0:c0 + m], res_y[:, c % 2, 0:m],
                                        ALU.add).then_inc(y_ready, 1)
                dve.wait_ge(y_ready, c + 1)
                nc.vector.bn_stats(stats[:, c, :], xT[0:F, c0:c0 + m]).then_inc(stats_ready, 1)
            dve.wait_ge(stats_ready, len(CHUNKS))
            nc.vector.bn_aggr(mv[:, :], stats[:, :, :].rearrange("f c s -> f (c s)")).then_inc(bn_step, 1)
            dve.wait_ge(bn_step, 2)
            nc.vector.reciprocal(affine[:, 1:2], affine[:, 0:1]).then_inc(bn_step, 1)
            dve.wait_ge(bn_step, 3)
            nc.vector.tensor_tensor(affine[:, 2:3], affine[:, 1:2], cols[:, 2:3], ALU.mult).then_inc(bn_step, 1)
            dve.wait_ge(bn_step, 4)
            nc.vector.tensor_tensor(affine[:, 3:4], mv[:, 0:1], affine[:, 2:3], ALU.mult).then_inc(bn_step, 1)
            nc.vector.tensor_scalar(affine[:, 5:6], affine[:, 2:3], 1.0 / F, None, ALU.mult).then_inc(bn_step, 1)
            dve.wait_ge(bn_step, 6)
            nc.vector.tensor_tensor(affine[:, 4:5], cols[:, 3:4], affine[:, 3:4], ALU.subtract).then_inc(bn_step, 1)
            dve.wait_ge(bn_step, 7)
            nc.vector.tensor_scalar(shift_diag[:, :], identity[:, :], affine[:, 4:5], None,
                                    ALU.mult).then_inc(bn_step, 1)
            nc.vector.tensor_scalar(combine[0:F, :], identity[:, :], affine[:, 2:3], affine[:, 5:6],
                                    ALU.mult, ALU.subtract).then_inc(bn_step, 1)
            nc.vector.tensor_scalar(combine[F:P, :], combine[F:P, :], 1.0 / F, None,
                                    ALU.subtract).then_inc(bn_step, 1)
            dve.wait_ge(shift_product, 1)
            nc.vector.tensor_reduce(shift_mean[:, :], psum[:, 0:F], AX.X, ALU.add).then_inc(shift_step, 1)
            dve.wait_ge(shift_step, 1)
            nc.vector.tensor_scalar(shift_mean[:, :], shift_mean[:, :], 1.0 / F, None, ALU.mult).then_inc(shift_step, 1)
            dve.wait_ge(shift_step, 2)
            nc.vector.tensor_scalar(shift_row[:, :], psum[:, 0:F], shift_mean[:, 0:1], None,
                                    ALU.subtract).then_inc(shift_step, 1)
            dve.wait_ge(shift_step, 3)
            for b in range(len(BLOCKS) + 2):
                if b < len(BLOCKS):
                    _, m, k = BLOCKS[b]
                    at = (4 + b % 2) * BANK
                    dve.wait_ge(z_product, b + 1)
                    if b >= ZS:
                        dve.wait_ge(z_stored[b % ZS], 16 * (b // ZS))
                    nc.vector.tensor_tensor(z_buf[0:m, b % ZS, 0:k * F].rearrange("p (k f) -> p k f", k=k),
                                            psum[0:m, at:at + k * F].rearrange("p (k f) -> p k f", k=k),
                                            shift_row[0:m, :].unsqueeze(1).broadcast_to([m, k, F]),
                                            ALU.add).then_inc(z_shifted, 1)
                if 1 <= b <= len(BLOCKS):
                    _, m, k = BLOCKS[b - 1]
                    dve.wait_ge(z_squared, b)
                    nc.vector.tensor_reduce(deviation[0:m, (b - 1) % ZS, 0, 0:k],
                                            squares[0:m, (b - 1) % 2, 0:k * F].rearrange("p (k f) -> p k f", k=k),
                                            AX.X, ALU.add).then_inc(var_ready, 1)
                if b >= 2:
                    _, m, k = BLOCKS[b - 2]
                    s = (b - 2) % ZS
                    dve.wait_ge(std_ready, b - 1)
                    nc.vector.reciprocal(deviation[0:m, s, 1, 0:k], deviation[0:m, s, 0, 0:k]).then_inc(inverse_ready, 1)
                    dve.wait_ge(inverse_ready, b - 1)
                    z = z_buf[0:m, s, 0:k * F].rearrange("p (k f) -> p k f", k=k)
                    nc.vector.tensor_tensor(z, z, deviation[0:m, s, 1, 0:k].unsqueeze(2).broadcast_to([m, k, F]),
                                            ALU.mult).then_inc(z_ready, 1)


def kernel(x, src, dst, edge_type_64, edge_weight1, L0_gnn_basis, L0_gnn_comp, L0_gnn_bias, L0_gnn_res_w,
           L0_gnn_res_b, L0_gnn_gamma, L0_gnn_beta):
    import numpy as np
    import concourse.bacc as bacc
    from concourse.bass_utils import run_bass_kernel_spmd

    def tile_columns(a):
        a = np.asarray(a).reshape(-1)
        padded = np.zeros(TILE_COLUMNS * P, a.dtype)
        padded[:N_EDGES] = a
        return np.ascontiguousarray(padded.reshape(TILE_COLUMNS, P).T)

    def column(a):
        return np.ascontiguousarray(np.asarray(a).reshape(F, 1))

    xT = np.zeros((F, NODES_PADDED), np.float32)
    xT[:, :N_NODES] = np.asarray(x).T
    basis = np.asarray(L0_gnn_basis).transpose(0, 2, 1)
    arrays = {
        "x_rows": np.ascontiguousarray(np.asarray(x)),
        "x2T": np.concatenate([xT, xT], axis=0),
        "src_cols": tile_columns(src),
        "type_cols": tile_columns(edge_type_64),
        "dst_cols": tile_columns(dst),
        "dst_flat": np.ascontiguousarray(np.asarray(dst)),
        "weight_cols": tile_columns(edge_weight1),
        "basis2": np.ascontiguousarray(np.concatenate([basis, basis], axis=2)),
        "compT": np.ascontiguousarray(np.asarray(L0_gnn_comp).T),
        "bias_col": column(L0_gnn_bias),
        "res_wT": np.ascontiguousarray(np.asarray(L0_gnn_res_w).T),
        "res_b_col": column(L0_gnn_res_b),
        "gamma_col": column(L0_gnn_gamma),
        "beta_col": column(L0_gnn_beta),
    }
    nc = bacc.Bacc("TRN2", target_bir_lowering=False, num_devices=1)
    args = {name: nc.dram_tensor(name, a.shape, mybir.dt.from_np(a.dtype), kind="ExternalInput").ap()
            for name, a in arrays.items()}
    out = nc.dram_tensor("out", (N_NODES, F), mybir.dt.float32, kind="ExternalOutput").ap()
    gnn_program(nc, out=out, **args)
    result = run_bass_kernel_spmd(nc, [arrays], core_ids=[0])
    return result.results[0]["out"]
```

```python
import concourse.bass as bass
from concourse import mybir
from contextlib import ExitStack

P = 128
N_NODES = 12500
N_EDGES = 200000
F = 64
RELS = 64
BASES = 64
BN_EPS = 1e-05
LN_EPS = 1e-05

NODE_TILES = -(-N_NODES // P)
NODES_PADDED = NODE_TILES * P
ROW = RELS * F
UNIT = 1024
UNITS = ROW // UNIT
BANK = 512

GROUP = 4
EDGE_TILES = -(-N_EDGES // P)
LAST_TILE_ROWS = N_EDGES - (EDGE_TILES - 1) * P
GROUPS = -(-EDGE_TILES // GROUP)
QUADS = 4
SLOTS = GROUP * QUADS
ALL_TURNS = GROUPS // QUADS
TILE_COLUMNS = (GROUPS + QUADS - 1) * GROUP

PAIR = 2
DIRECT_PER_TURN = PAIR * QUADS
TURNS = EDGE_TILES // (SLOTS + DIRECT_PER_TURN)
DIRECT_TILES = TURNS * DIRECT_PER_TURN
FIRST_GROUP = DIRECT_TILES // GROUP
RING = 4
RING_AT = 2 * ROW
ROWS_AT = RING_AT + RING * DIRECT_PER_TURN * F
BEHIND = 2
FOUND_LAP = 3
FLAG_LAP = 8
KEY_TURN = 12
RES_CHUNKS = TURNS - 1
RES_NODES = NODES_PADDED // RES_CHUNKS
assert DIRECT_TILES % GROUP == 0 and TURNS % RING == 1 and RES_NODES * RES_CHUNKS == NODES_PADDED
assert 0 <= GROUPS - FIRST_GROUP - TURNS * QUADS < QUADS

WINDOW = 128
NARROW = 8
KEYS = NARROW * RELS
REL_PAIRS = RELS // 2
WIDE = 512
WIDE_WINDOWS = -(-N_NODES // WIDE)
H_COLUMNS = max(WIDE_WINDOWS * WIDE, N_NODES + WINDOW)

GP = 78
GJ = (GROUPS - 1) // GP
GE = GROUP * P
LAST_EDGES = N_EDGES - (GROUPS - 1) * GE

BN_STEPS = 10
CHUNKS = [(c, min(BANK, N_NODES - c)) for c in range(0, N_NODES, BANK)]
K8 = 8
BLOCKS = [(b, P, K8) for b in range(0, N_NODES - P * K8 + 1, P * K8)]
REST = N_NODES - len(BLOCKS) * P * K8
RK = 4
ZS = 6
BLOCKS.append((len(BLOCKS) * P * K8, REST // RK, RK))


def gnn_program(nc, x_rows, x2T, src_cols, type_cols, dst_cols, dst_flat, weight_cols, basis2, compT,
                bias_col, res_wT, res_b_col, gamma_col, beta_col, out):
    f32, bf16, i32 = mybir.dt.float32, mybir.dt.bfloat16, mybir.dt.int32
    ALU, ACT, AX = mybir.AluOpType, mybir.ActivationFunctionType, mybir.AxisListType

    ctx = ExitStack()
    with ctx:
        def sb(name, shape, dt):
            return ctx.enter_context(nc.sbuf_tensor(name, shape, dt))

        def sem(name):
            return ctx.enter_context(nc.semaphore(name))

        table = nc.dram_tensor("message_table", [NODES_PADDED * RELS, F], f32).ap()
        table_tiles = table.rearrange("(t p r) o -> t p (r o)", p=P, r=RELS)
        base_dram = nc.dram_tensor("group_base", [GROUPS], i32).ap()
        span_dram = nc.dram_tensor("group_span", [GROUPS], i32).ap()
        direct_base_dram = nc.dram_tensor("direct_base", [DIRECT_TILES], i32).ap()
        direct_span_dram = nc.dram_tensor("direct_span", [DIRECT_TILES], i32).ap()
        x_direct = nc.dram_tensor("x_direct", [TURNS, P, DIRECT_PER_TURN * F], f32).ap()

        xT = sb("xT", [P, NODES_PADDED], f32)
        h_arena = sb("h_arena", [P, H_COLUMNS], f32)
        hT = h_arena[0:F, :]
        basis_sb = h_arena[:, 0:ROW].rearrange("b (o i) -> b o i", i=2 * F)
        w_f32 = h_arena[:, ROW:2 * ROW]
        y_stage = sb("y_stage", [P, 2 * UNITS * UNIT], f32)
        type_i = y_stage[:, 0:TILE_COLUMNS].bitcast(i32)
        dst_i = y_stage[:, TILE_COLUMNS:2 * TILE_COLUMNS].bitcast(i32)
        direct_rows = h_arena[:, RING_AT:ROWS_AT].rearrange(
            "p (s k f) -> p s k f", s=RING, k=DIRECT_PER_TURN)
        dst_rows = h_arena[0:GP, ROWS_AT:ROWS_AT + GJ * GE].bitcast(i32)
        w_rem = h_arena[:, 0:UNIT]
        pair_sums = y_stage[:, 0:REL_PAIRS * 64].rearrange("p (r c) -> p r c", r=REL_PAIRS)
        select = y_stage[:, 2048:3072].rearrange("p (s k n) -> p s k n", s=2, k=GROUP)
        pair_select = y_stage[:, 3072:4096].bitcast(bf16).rearrange("p (s j c) -> p s j c", s=2, j=PAIR)
        direct_x = y_stage[:, 4096:4608].rearrange("p (q c) -> p q c", q=QUADS)
        scaled = y_stage[:, 4608:4864].rearrange("p (s c) -> p s c", s=2)
        scaled_rem = y_stage[:, 4864:5120].rearrange("p (s c) -> p s c", s=2)
        parts = y_stage[:, 5120:5504].bitcast(bf16).rearrange("p (t s c) -> p t s c", t=3, s=2)
        z_buf = y_stage[:, 0:6 * BANK].rearrange("p (s n) -> p s n", s=ZS)
        squares = y_stage[:, 6 * BANK:8 * BANK].rearrange("p (s n) -> p s n", s=2)

        stats = y_stage[0:F, 8 * BANK:8 * BANK + 6 * len(CHUNKS)].rearrange("f (c s) -> f c s", s=6)
        shift_row = y_stage[:, 9 * BANK:9 * BANK + F]
        shift_diag = y_stage[0:F, 9 * BANK + F:9 * BANK + 2 * F]

        w_high = sb("w_high", [P, ROW], bf16)
        w_mid = sb("w_mid", [P, ROW], bf16)
        w_lowhigh = sb("w_lowhigh", [P, ROW], bf16)
        wide_select = w_high[:, :].bitcast(f32).rearrange("p (k n) -> p k n", k=GROUP)
        wide_iota = w_mid[:, 0:2 * WIDE].bitcast(f32)
        w_pairs = sb("w_pairs", [P, REL_PAIRS, F], f32)
        x_hm = sb("x_hm", [P, 2, P], bf16)
        x_hl = sb("x_hl", [P, 2, P], bf16)
        x_rem = sb("x_rem", [P, 2, P], f32)

        row_index = sb("row_index", [P, TILE_COLUMNS], i32)
        dst_key = sb("dst_key", [P, TILE_COLUMNS], f32)
        weight = sb("weight", [P, TILE_COLUMNS], f32)
        gathered_rows = sb("gathered_rows", [P, SLOTS, F], f32)
        base_row = sb("base_row", [P, GROUPS], i32)
        dst_last = base_row[0:1, 0:LAST_EDGES]
        dst_direct = gathered_rows[0:TURNS, :, :].rearrange("p s f -> p (s f)")[:, 0:DIRECT_PER_TURN * P].bitcast(i32)
        span_row = sb("span_row", [1, GROUPS], i32)
        direct_src = sb("direct_src", [P, DIRECT_TILES], i32)
        direct_key = sb("direct_key", [P, DIRECT_TILES], f32)
        direct_base_row = sb("direct_base_row", [P, DIRECT_TILES], i32)
        direct_span_row = sb("direct_span_row", [1, DIRECT_TILES], i32)
        span_max = sb("span_max", [1, 2], i32)
        relative = h_arena[:, 0:DIRECT_TILES]
        base_g = sb("base_g", [GP, GJ], i32)
        span_g = sb("span_g", [GP, GJ], i32)
        last_bs = sb("last_bs", [1, 2], i32)
        base_d = sb("base_d", [TURNS, DIRECT_PER_TURN], i32)
        span_d = sb("span_d", [TURNS, DIRECT_PER_TURN], i32)
        direct_index = sb("direct_index", [P, RING, DIRECT_PER_TURN], i32)
        comp_sb = sb("comp_sb", [P, P], f32)
        cols = sb("cols", [F, 4], f32)
        res_w = sb("res_w", [P, F], f32)

        index_slot = sb("index_slot", [P, SLOTS], i32)
        node_iota = sb("node_iota", [P, WIDE], f32)
        key_iota = sb("key_iota", [P, KEYS], f32)

        mv = sb("mv", [F, 2], f32)
        affine = sb("affine", [F, 6], f32)
        identity = sb("identity", [F, F], f32)
        combine = sb("combine", [P, F], f32)
        ones = sb("ones", [F, P], f32)
        eps_col = sb("eps_col", [P, 1], f32)
        shift_mean = sb("shift_mean", [P, 1], f32)
        deviation = sb("deviation", [P, ZS, 2, K8], f32)

        psum = ctx.enter_context(nc.psum_tensor("psum", [P, 8 * BANK], f32))

        wait_carrier = sem("wait_carrier")
        s_x = sem("s_x")
        s_basis = sem("s_basis")
        s_comp = sem("s_comp")
        comp_zeroed = sem("comp_zeroed")
        w_high_ready = sem("w_high_ready")
        s_x_rest = sem("s_x_rest")
        s_edges = sem("s_edges")
        s_direct_src = sem("s_direct_src")
        direct_copied = sem("direct_copied")
        direct_gathered = [sem(f"direct_gathered_{s}") for s in range(RING * DIRECT_PER_TURN)]
        direct_stored = [sem(f"direct_stored_{s}") for s in range(RING)]
        direct_loaded = [sem(f"direct_loaded_{q}") for q in range(QUADS)]
        pair_scaled = sem("pair_scaled")
        pair_selected = sem("pair_selected")
        pair_high = sem("pair_high")
        pair_rem = sem("pair_rem")
        pair_mid = sem("pair_mid")
        pair_low = sem("pair_low")
        pairs_summed = sem("pairs_summed")
        pairs_evacuated = sem("pairs_evacuated")
        transformed = sem("transformed")
        tile_added = sem("tile_added")
        turns_added = sem("turns_added")
        s_weight = sem("s_weight")
        s_rows = sem("s_rows")
        s_cols = sem("s_cols")
        s_resw = sem("s_resw")
        bases_found = sem("bases_found")
        bases_stored = sem("bases_stored")
        bases_loaded = sem("bases_loaded")
        flag_ready = sem("flag_ready")
        w_product = sem("w_product")
        w_copied = sem("w_copied")
        w_parts = sem("w_parts")
        x_parts = sem("x_parts")
        x_step = sem("x_step")
        unit_full = sem("unit_full")
        act_free = sem("act_free")
        dve_free = sem("dve_free")
        dve_step = sem("dve_step")
        stored = [sem(f"stored_{s}") for s in range(2 * UNITS)]
        edges_used = sem("edges_used")
        h_zeroed = sem("h_zeroed")
        keys_made = sem("keys_made")
        key_unshifted = sem("key_unshifted")
        iota_step = sem("iota_step")
        constants = sem("constants")
        index_ready = sem("index_ready")
        gathered = [sem(f"gathered_{s}") for s in range(SLOTS)]
        select_ready = sem("select_ready")
        window_summed = sem("window_summed")
        sum_free = sem("sum_free")
        h_done = sem("h_done")
        res_product = sem("res_product")
        res_free = sem("res_free")
        relu_ready = sem("relu_ready")
        y_ready_dve = sem("y_ready_dve")
        y_ready_pool = sem("y_ready_pool")
        stats_ready = sem("stats_ready")
        bn_step = sem("bn_step")
        shift_product = sem("shift_product")
        shift_step = sem("shift_step")
        z_product = sem("z_product")
        z_shifted = sem("z_shifted")
        z_squared = sem("z_squared")
        var_ready = sem("var_ready")
        std_ready = sem("std_ready")
        inverse_ready = sem("inverse_ready")
        z_ready_even = sem("z_ready_even")
        z_ready_odd = sem("z_ready_odd")
        z_stored = [sem(f"z_stored_{s}") for s in range(ZS)]

        block = ctx.enter_context(nc.Block())

        def unit_psum(u):
            return psum[:, u * UNIT:(u + 1) * UNIT]

        def stage(t, u):
            s = (t % 2) * UNITS + u
            return y_stage[:, s * UNIT:(s + 1) * UNIT]

        def wait(engine, semaphore, value):
            if not isinstance(value, int) or value > 0:
                engine.wait_ge(semaphore, value)

        def modes(engine):
            engine.wait_ge(flag_ready, 1)
            group_span = engine.value_load(span_max[0:1, 0:1], min_val=0, max_val=N_NODES)
            direct_span = engine.value_load(span_max[0:1, 1:2], min_val=0, max_val=2 * N_NODES)
            return group_span, direct_span

        def table_stored(engine):
            for s in range(2 * UNITS):
                engine.wait_ge(stored[s], 16 * (NODE_TILES // 2))

        @block.sync
        def _(sp):
            sp.dma_start(basis_sb, basis2).then_inc(s_basis, 16)
            sp.dma_start(xT[:, 0:2 * P], x2T[:, 0:2 * P]).then_inc(s_x, 16)
            sp.dma_start(type_i, type_cols).then_inc(s_edges, 16)
            sp.dma_start(dst_i, dst_cols).then_inc(s_edges, 16)
            sp.dma_start(row_index[:, :], src_cols).then_inc(s_edges, 16)
            sp.dma_start(xT[:, 2 * P:NODES_PADDED], x2T[:, 2 * P:NODES_PADDED]).then_inc(s_x_rest, 16)
            sp.dma_start(dst_rows, dst_flat[0:GP * GJ * GE].rearrange("(p n) -> p n", p=GP)).then_inc(s_rows, 16)
            sp.dma_start(dst_last, dst_flat[GP * GJ * GE:N_EDGES].unsqueeze(0)).then_inc(s_rows, 16)
            sp.dma_start(dst_direct, dst_flat[0:DIRECT_TILES * P].rearrange("(p n) -> p n", p=TURNS)).then_inc(s_rows, 16)
            sp.dma_start(weight[:, :], weight_cols).then_inc(s_weight, 16)
            with sp.Fori(0, NODE_TILES // 2) as i:
                for t in range(2):
                    for u in range(UNITS):
                        sp.wait_ge(act_free if u % 2 == 0 else dve_free, 4 * i + 2 * t + u // 2 + 3)
                        sp.dma_start(table_tiles[2 * i + t, :, u * UNIT:(u + 1) * UNIT],
                                     stage(t, u)).then_inc(stored[t * UNITS + u], 16)
            table_stored(sp)
            for s in range(RING):
                sp.wait_ge(direct_stored[s], 16 * len(range(s, TURNS, RING)))
            group_span, direct_span = modes(sp)
            with sp.If((group_span < WINDOW) & (direct_span < NARROW)):
                def load_direct(i):
                    for q in range(QUADS):
                        wait(sp, pair_scaled, QUADS * (i - 1) + q + 1)
                        sp.dma_start(direct_x[:, q, :], x_direct[i, :, q * PAIR * F:(q + 1) * PAIR * F]
                                     ).then_inc(direct_loaded[q], 16)

                load_direct(0)
                with sp.Fori(1, TURNS) as i:
                    load_direct(i)
            for b, (n0, m, k) in enumerate(BLOCKS):
                sp.wait_ge(z_ready_even if b % 2 == 0 else z_ready_odd, b // 2 + 1)
                sp.dma_start(out[n0:n0 + m * k, :].rearrange("(p k) f -> p (k f)", k=k),
                             z_buf[0:m, b % ZS, 0:k * F]).then_inc(z_stored[b % ZS], 16)
            for s in range(ZS):
                sp.wait_ge(z_stored[s], 16 * len(range(s, len(BLOCKS), ZS)))

        @block.gpsimd
        def _(pool):
            nc.gpsimd.iota(node_iota[:, :], [[1, WIDE]], base=0, channel_multiplier=0,
                           allow_small_or_imprecise_dtypes=True).then_inc(constants, 1)
            nc.gpsimd.iota(key_iota[:, :], [[1, 2], [RELS, NARROW], [2, REL_PAIRS]], base=0, channel_multiplier=0,
                           allow_small_or_imprecise_dtypes=True).then_inc(constants, 1)
            nc.gpsimd.memset(combine[:, :], 0.0).then_inc(constants, 1)
            nc.gpsimd.memset(identity[:, :], 0.0).then_inc(constants, 1)
            nc.gpsimd.memset(ones[:, :], 1.0).then_inc(constants, 1)
            nc.gpsimd.memset(eps_col[:, :], BN_EPS).then_inc(constants, 1)
            pool.wait_ge(constants, 7)
            nc.gpsimd.affine_select(out=identity[:, :], in_=identity[:, :], compare_op=ALU.not_equal, fill=1.0,
                                    base=0, pattern=[[-1, F]], channel_multiplier=1).then_inc(constants, 1)
            nc.gpsimd.affine_select(out=combine[:, :], in_=combine[:, :], compare_op=ALU.not_equal, fill=1.0,
                                    base=-F, pattern=[[-1, F]], channel_multiplier=1).then_inc(constants, 1)
            pool.wait_ge(s_direct_src, 16)

            def gather_direct(b, s, lap):
                wait(pool, direct_stored[s], 16 * lap)
                nc.gpsimd.tensor_copy(direct_index[:, s, :],
                                      direct_src[:, bass.ds(b * DIRECT_PER_TURN, DIRECT_PER_TURN)]
                                      ).then_inc(direct_copied, 1)
                pool.wait_ge(direct_copied, b + 1)
                pool.sem_inc(wait_carrier, 1)
                for k in range(DIRECT_PER_TURN):
                    pool.indirect_dma_start(
                        out=direct_rows[:, s, k, :], out_offset=None, in_=x_rows,
                        in_offset=bass.IndirectOffsetOnAxis(ap=direct_index[:, s, k:k + 1], axis=0),
                    ).then_inc(direct_gathered[s * DIRECT_PER_TURN + k], 16)

            def store_direct(b, s, lap):
                for k in range(DIRECT_PER_TURN):
                    pool.wait_ge(direct_gathered[s * DIRECT_PER_TURN + k], 16 * (lap + 1))
                pool.sem_inc(wait_carrier, 1)
                pool.dma_start(x_direct[b, :, :], direct_rows[:, s, :, :].rearrange("p k f -> p (k f)")
                               ).then_inc(direct_stored[s], 16)

            for b in range(RING):
                gather_direct(b, b, 0)
                if b >= BEHIND:
                    store_direct(b - BEHIND, b - BEHIND, 0)

            def laps(first, last):
                with pool.Fori(first, last) as lap:
                    for s in range(RING):
                        gather_direct(RING * lap + s, s, lap)
                        store_direct(RING * lap + s - BEHIND, (s - BEHIND) % RING, lap if s >= BEHIND else lap - 1)

            laps(1, FOUND_LAP)
            pool.wait_ge(bases_found, 1)
            pool.dma_start(base_dram[0:GP * GJ].rearrange("(p n) -> p n", p=GP), base_g[:, :]).then_inc(bases_stored, 16)
            pool.dma_start(span_dram[0:GP * GJ].rearrange("(p n) -> p n", p=GP), span_g[:, :]).then_inc(bases_stored, 16)
            pool.dma_start(base_dram[GP * GJ:GROUPS].unsqueeze(0), last_bs[:, 0:1]).then_inc(bases_stored, 16)
            pool.dma_start(span_dram[GP * GJ:GROUPS].unsqueeze(0), last_bs[:, 1:2]).then_inc(bases_stored, 16)
            pool.dma_start(direct_base_dram.rearrange("(p n) -> p n", p=TURNS), base_d[:, :]).then_inc(bases_stored, 16)
            pool.dma_start(direct_span_dram.rearrange("(p n) -> p n", p=TURNS), span_d[:, :]).then_inc(bases_stored, 16)
            pool.wait_ge(bases_stored, 96)
            pool.dma_start(base_row[:, :], base_dram.partition_broadcast(P)).then_inc(bases_loaded, 16)
            pool.dma_start(span_row[:, :], span_dram.unsqueeze(0)).then_inc(bases_loaded, 16)
            pool.dma_start(direct_base_row[:, :], direct_base_dram.partition_broadcast(P)).then_inc(bases_loaded, 16)
            pool.dma_start(direct_span_row[:, :], direct_span_dram.unsqueeze(0)).then_inc(bases_loaded, 16)
            laps(FOUND_LAP, FLAG_LAP)
            pool.wait_ge(flag_ready, 1)
            pool.wait_ge(w_copied, 4)
            nc.gpsimd.memset(hT[:, 0:RING_AT], 0.0).then_inc(h_zeroed, 1)
            nc.gpsimd.memset(hT[:, ROWS_AT:H_COLUMNS], 0.0).then_inc(h_zeroed, 1)
            laps(FLAG_LAP, TURNS // RING)
            for b in range(TURNS // RING * RING, TURNS + BEHIND):
                if b < TURNS:
                    gather_direct(b, b % RING, b // RING)
                store_direct(b - BEHIND, (b - BEHIND) % RING, (b - BEHIND) // RING)
            for s in range(RING):
                pool.wait_ge(direct_stored[s], 16 * len(range(s, TURNS, RING)))
            nc.gpsimd.memset(hT[:, RING_AT:ROWS_AT], 0.0).then_inc(h_zeroed, 1)
            for s in range(2 * UNITS):
                pool.wait_ge(stored[s], 16 * (NODE_TILES // 2))

            def gather(slot, rows=P):
                pool.indirect_dma_start(
                    out=gathered_rows[0:rows, slot, :], out_offset=None, in_=table,
                    in_offset=bass.IndirectOffsetOnAxis(ap=index_slot[0:rows, slot:slot + 1], axis=0),
                ).then_inc(gathered[slot], 16)

            def gather_groups(first, turns):
                with pool.Fori(0, turns) as i:
                    for q in range(QUADS):
                        pool.wait_ge(index_ready, QUADS * i + q + 1)
                        pool.sem_inc(wait_carrier, 1)
                        for k in range(GROUP):
                            gather(q * GROUP + k)
                for n in range(turns * QUADS, GROUPS - first):
                    pool.wait_ge(index_ready, n + 1)
                    for k in range(GROUP):
                        tile = (first + n) * GROUP + k
                        if tile < EDGE_TILES:
                            gather(n % QUADS * GROUP + k, P if tile < EDGE_TILES - 1 else LAST_TILE_ROWS)

            group_span, direct_span = modes(pool)
            with pool.If((group_span < WINDOW) & (direct_span < NARROW)):
                gather_groups(FIRST_GROUP, TURNS)
            with pool.Else():
                gather_groups(0, ALL_TURNS)
            pool.wait_ge(h_done, 1)
            pool.wait_ge(res_free, RES_CHUNKS + 1)
            for c, (c0, m) in enumerate(CHUNKS):
                if c % 3 != 0:
                    pool.wait_ge(relu_ready, c + 1)
                    nc.gpsimd.tensor_tensor(xT[0:F, c0:c0 + m], hT[:, c0:c0 + m], xT[0:F, c0:c0 + m],
                                            ALU.add).then_inc(y_ready_pool, 1)
            for b, (_, m, k) in enumerate(BLOCKS):
                if b % 2 == 1:
                    s = b % ZS
                    pool.wait_ge(inverse_ready, b + 1)
                    z = z_buf[0:m, s, 0:k * F].rearrange("p (k f) -> p k f", k=k)
                    nc.gpsimd.tensor_tensor(z, z, deviation[0:m, s, 1, 0:k].unsqueeze(2).broadcast_to([m, k, F]),
                                            ALU.mult).then_inc(z_ready_odd, 1)

        @block.tensor
        def _(pe):
            pe.wait_ge(s_basis, 16)
            pe.wait_ge(s_comp, 32)
            for o in range(F // 2):
                last = nc.tensor.matmul(psum[:, 2 * o * RELS:2 * (o + 1) * RELS], basis_sb[:, o, :], comp_sb[:, :],
                                        start=True, stop=True)
            last.then_inc(w_product, 1)
            pe.wait_ge(w_copied, 2)
            with pe.Fori(0, NODE_TILES // 2) as i:
                for t in range(2):
                    pe.wait_ge(x_parts, 2 * i + t + 1)
                    for u in range(UNITS):
                        pe.wait_ge(w_parts, u + 1)
                        pe.wait_ge(act_free if u % 2 == 0 else dve_free, 4 * i + 2 * t + u // 2 + 1)
                        for c in range(2 * u, 2 * u + 2):
                            at = slice(c * BANK, (c + 1) * BANK)
                            nc.tensor.matmul(psum[:, at], x_hl[:, t, :], w_lowhigh[:, at], start=True, stop=False)
                            nc.tensor.matmul(psum[:, at], x_hm[:, t, :], w_mid[:, at], start=False, stop=False)
                            last = nc.tensor.matmul(psum[:, at], x_hm[:, t, :], w_high[:, at], start=False, stop=True)
                        last.then_inc(unit_full, 1)
            pe.wait_ge(act_free, 2 * NODE_TILES + 2)
            pe.wait_ge(dve_free, 2 * NODE_TILES + 2)

            def sum_group(q, turn, rhs, width, ready, free, tiles=GROUP, last_rows=P):
                pe.wait_ge(select_ready, ready)
                pe.wait_ge(sum_free, free)
                for k in range(tiles):
                    slot = q * GROUP + k
                    rows = last_rows if k == tiles - 1 else P
                    pe.wait_ge(gathered[slot], 16 * (turn + 1))
                    last = nc.tensor.matmul(psum[0:F, q * BANK:q * BANK + width], gathered_rows[0:rows, slot, :],
                                            rhs(k, rows), start=(k == 0), stop=(k == tiles - 1))
                last.then_inc(window_summed, 1)

            def tail(g):
                tiles = min(GROUP, EDGE_TILES - g * GROUP)
                return dict(tiles=tiles, last_rows=LAST_TILE_ROWS if g == GROUPS - 1 else P)

            def narrow(q):
                return lambda k, rows: select[0:rows, q % 2, k, :]

            def wide(k, rows):
                return wide_select[0:rows, k, :]

            def sum_pair(n, q):
                pe.wait_ge(pair_selected, n + 1)
                pe.wait_ge(pair_low, n + 1)
                wait(pe, pairs_evacuated, n - 1)
                bank = (QUADS + q % 2) * BANK
                half = KEYS // 2
                for j in range(PAIR):
                    for part in range(3):
                        for parity in range(2):
                            last = nc.tensor.matmul(
                                psum[parity * F:(parity + 1) * F, bank + j * half:bank + (j + 1) * half],
                                parts[:, part, q % 2, j * F:(j + 1) * F],
                                pair_select[:, q % 2, j, parity * half:(parity + 1) * half],
                                start=(part == 0), stop=(part == 2))
                last.then_inc(pairs_summed, 1)

            def transform(i, half):
                if half == 0:
                    pe.wait_ge(pairs_evacuated, QUADS * (i + 1))
                    pe.wait_ge(turns_added, i + 1)
                for r in range(half * REL_PAIRS // 2, (half + 1) * REL_PAIRS // 2):
                    last = nc.tensor.matmul(psum[0:F, 6 * BANK:6 * BANK + DIRECT_PER_TURN * NARROW], w_pairs[:, r, :],
                                            pair_sums[:, r, :], start=(r == 0), stop=(r == REL_PAIRS - 1))
                if half == 1:
                    last.then_inc(transformed, 1)

            def res_chunk(i):
                pe.wait_ge(res_free, i)
                nc.tensor.matmul(psum[0:F, 7 * BANK:7 * BANK + RES_NODES], res_w[:, :],
                                 xT[:, bass.ds((i - 1) * RES_NODES, RES_NODES)],
                                 start=True, stop=True).then_inc(res_product, 1)

            pe.wait_ge(s_resw, 16)
            pe.wait_ge(constants, 9)
            group_span, direct_span = modes(pe)
            with pe.If((group_span < WINDOW) & (direct_span < NARROW)):
                def both(i):
                    for q in range(QUADS):
                        n = QUADS * i + q
                        sum_group(q, i, narrow(q), WINDOW, n + 1, n + 1)
                        if q < 2 and not (isinstance(i, int) and i == 0):
                            transform(i - 1, q)
                        sum_pair(n, q)

                both(0)
                with pe.Fori(1, TURNS) as i:
                    both(i)
                    res_chunk(i)
                for n in range(TURNS * QUADS, GROUPS - FIRST_GROUP):
                    sum_group(n % QUADS, n // QUADS, narrow(n % QUADS), WINDOW, n + 1, n + 1, **tail(FIRST_GROUP + n))
                transform(TURNS - 1, 0)
                transform(TURNS - 1, 1)
            with pe.Else():
                with pe.Fori(1, TURNS) as i:
                    res_chunk(i)
                with pe.If(group_span < WINDOW):
                    with pe.Fori(0, ALL_TURNS) as i:
                        for q in range(QUADS):
                            n = QUADS * i + q + 1
                            sum_group(q, i, narrow(q), WINDOW, n, n)
                    for g in range(ALL_TURNS * QUADS, GROUPS):
                        sum_group(g % QUADS, g // QUADS, narrow(g % QUADS), WINDOW, g + 1, g + 1, **tail(g))
                with pe.Else():
                    with pe.Fori(0, ALL_TURNS) as i:
                        for q in range(QUADS):
                            with pe.Fori(0, WIDE_WINDOWS) as w:
                                n = (QUADS * i + q) * WIDE_WINDOWS + w + 1
                                sum_group(q, i, wide, WIDE, n, n + QUADS - 1)
                    for g in range(ALL_TURNS * QUADS, GROUPS):
                        with pe.Fori(0, WIDE_WINDOWS) as w:
                            n = g * WIDE_WINDOWS + w + 1
                            sum_group(g % QUADS, g // QUADS, wide, WIDE, n, n + QUADS - 1, **tail(g))
                pe.sem_inc(wait_carrier, 1)
            pe.wait_ge(bn_step, BN_STEPS)
            nc.tensor.matmul(psum[:, 0:F], ones[:, :], shift_diag[:, :], start=True, stop=True).then_inc(shift_product, 1)
            for b, (n0, m, k) in enumerate(BLOCKS):
                if b >= 2:
                    pe.wait_ge(z_shifted, b - 1)
                for j in range(k):
                    at = (4 + 2 * (b % 2)) * BANK + j * 2 * F
                    last = nc.tensor.matmul(psum[0:m, at:at + 2 * F].rearrange("p (s f) -> p s f", s=2),
                                            xT[:, n0 + j:n0 + j + (m - 1) * k + 1:k],
                                            combine[:, :].unsqueeze(1).broadcast_to([P, 2, F]), start=True, stop=True)
                last.then_inc(z_product, 1)

        @block.scalar
        def _(act):
            act.wait_ge(comp_zeroed, 1)
            act.dma_start(comp_sb[0:BASES, 0:RELS], compT).then_inc(s_comp, 16)
            act.dma_start(comp_sb[BASES:P, RELS:P], compT).then_inc(s_comp, 16)
            act.dma_start(direct_src[:, :], src_cols[:, 0:DIRECT_TILES]).then_inc(s_direct_src, 16)
            act.dma_start(cols[:, 0:1], bias_col).then_inc(s_cols, 16)
            act.dma_start(cols[:, 1:2], res_b_col).then_inc(s_cols, 16)
            act.dma_start(cols[:, 2:3], gamma_col).then_inc(s_cols, 16)
            act.dma_start(cols[:, 3:4], beta_col).then_inc(s_cols, 16)
            act.dma_start(res_w[0:F, :], res_wT).then_inc(s_resw, 16)
            act.wait_ge(w_product, 1)
            w_out = w_f32.rearrange("p (r o) -> p o r", o=F)
            w_in = psum[:, :].rearrange("p (o r) -> p o r", r=RELS)
            nc.scalar.copy(w_out[:, 0:F // 2, :], w_in[:, 0:F // 2, :]).then_inc(w_copied, 1)
            act.wait_ge(w_copied, 2)
            for u in range(UNITS):
                at = slice(u * UNIT, (u + 1) * UNIT)
                nc.scalar.copy(w_high[:, at], w_f32[:, at]).then_inc(w_high_ready, 1)
                nc.scalar.copy(w_lowhigh[F:P, at], w_f32[F:P, at]).then_inc(w_high_ready, 1)
            act.sem_inc(act_free, 2)
            act.wait_ge(edges_used, 1)
            for peeled in (True, False):
                def evacuate(i):
                    for t in range(2):
                        for u in range(0, UNITS, 2):
                            act.wait_ge(unit_full, UNITS * (2 * i + t) + u + 1)
                            if not peeled:
                                act.wait_ge(stored[t * UNITS + u], 16 * i)
                            nc.scalar.copy(stage(t, u), unit_psum(u)).then_inc(act_free, 1)
                if peeled:
                    evacuate(0)
                    w_even_odd = w_f32.rearrange("p (r t o) -> p r t o", t=2, o=F)
                    nc.scalar.copy(w_pairs[0:F, :, :], w_even_odd[0:F, :, 0, :]).then_inc(w_copied, 1)
                    nc.scalar.copy(w_pairs[F:P, :, :], w_even_odd[F:P, :, 1, :]).then_inc(w_copied, 1)
                else:
                    with act.Fori(1, NODE_TILES // 2) as i:
                        evacuate(i)

            def evacuate_res(i):
                act.wait_ge(res_product, i)
                nc.scalar.activation(xT[0:F, bass.ds((i - 1) * RES_NODES, RES_NODES)],
                                     psum[0:F, 7 * BANK:7 * BANK + RES_NODES],
                                     ACT.Relu, bias=cols[:, 1:2]).then_inc(res_free, 1)

            act.wait_ge(s_cols, 64)
            act.sem_inc(res_free, 1)
            group_span, direct_span = modes(act)
            with act.If((group_span < WINDOW) & (direct_span < NARROW)):
                def split_pair(n, q):
                    act.wait_ge(pair_scaled, n + 1)
                    wait(act, pairs_summed, n - 1)
                    nc.scalar.copy(parts[:, 0, q % 2, :], scaled[:, q % 2, :]).then_inc(pair_high, 1)
                    act.wait_ge(pair_rem, n + 1)
                    nc.scalar.copy(parts[:, 1, q % 2, :], scaled_rem[:, q % 2, :]).then_inc(pair_mid, 1)

                def evacuate_pair(n, i, q):
                    act.wait_ge(pairs_summed, n + 1)
                    if q == 0:
                        wait(act, transformed, i)
                    bank = (QUADS + q % 2) * BANK
                    columns = PAIR * NARROW
                    nc.scalar.copy(
                        pair_sums[:, :, q * columns:(q + 1) * columns].rearrange("p r (j n) -> p j n r", j=PAIR),
                        psum[:, bank:bank + BANK].rearrange("p (j n r) -> p j n r", j=PAIR, n=NARROW),
                    ).then_inc(pairs_evacuated, 1)

                def pairs(i):
                    for q in range(QUADS):
                        n = QUADS * i + q
                        split_pair(n, q)
                        if q > 0:
                            evacuate_pair(n - 1, i, q - 1)
                        elif not (isinstance(i, int) and i == 0):
                            evacuate_pair(n - 1, i - 1, QUADS - 1)

                pairs(0)
                with act.Fori(1, TURNS) as i:
                    pairs(i)
                    evacuate_res(i)
                evacuate_pair(TURNS * QUADS - 1, TURNS - 1, QUADS - 1)
            with act.Else():
                with act.Fori(1, TURNS) as i:
                    evacuate_res(i)
            act.wait_ge(h_done, 1)
            for c, (c0, m) in enumerate(CHUNKS):
                nc.scalar.activation(hT[:, c0:c0 + m], hT[:, c0:c0 + m], ACT.Relu,
                                     bias=cols[:, 0:1]).then_inc(relu_ready, 1)
            act.wait_ge(bn_step, 1)
            nc.scalar.activation(affine[:, 0:1], mv[:, 1:2], ACT.Sqrt, bias=eps_col[0:F, :]).then_inc(bn_step, 1)
            for b in range(len(BLOCKS) + 1):
                if b < len(BLOCKS):
                    _, m, k = BLOCKS[b]
                    act.wait_ge(z_shifted, b + 1)
                    if b >= 2:
                        act.wait_ge(var_ready, b - 1)
                    nc.scalar.activation(squares[0:m, b % 2, 0:k * F], z_buf[0:m, b % ZS, 0:k * F],
                                         ACT.Square).then_inc(z_squared, 1)
                if b >= 1:
                    _, m, k = BLOCKS[b - 1]
                    act.wait_ge(var_ready, b)
                    sums = deviation[0:m, (b - 1) % ZS, 0, 0:k]
                    nc.scalar.activation(sums, sums, ACT.Sqrt, bias=eps_col[0:m, :],
                                         scale=1.0 / F).then_inc(std_ready, 1)

        @block.vector
        def _(dve):
            steps = [0]

            def step(instruction):
                steps[0] += 1
                instruction.then_inc(dve_step, 1)
                dve.wait_ge(dve_step, steps[0])

            nc.vector.memset(comp_sb[:, :], 0.0).then_inc(comp_zeroed, 1)
            nc.vector.memset(res_w[F:P, :], 0.0).then_inc(constants, 1)
            dve.wait_ge(s_edges, 48)
            nc.vector.scalar_tensor_tensor(out=row_index[:, :], in0=row_index[:, :], scalar=float(RELS),
                                           in1=type_i, op0=ALU.mult, op1=ALU.add).then_inc(dve_step, 1)
            nc.vector.tensor_copy(dst_key[:, :], dst_i).then_inc(dve_step, 1)
            nc.vector.tensor_copy(direct_key[:, :], type_i[:, 0:DIRECT_TILES]).then_inc(dve_step, 1)
            steps[0] = 3
            dve.wait_ge(dve_step, 3)
            dve.sem_inc(edges_used, 1)

            def find_bases():
                dve.wait_ge(s_rows, 48)
                grouped = dst_rows.rearrange("p (g e) -> p g e", g=GJ)
                direct = dst_direct.rearrange("p (t e) -> p t e", t=DIRECT_PER_TURN)
                for least, most, targets in ((base_g[:, :], span_g[:, :], grouped), (base_d[:, :], span_d[:, :], direct),
                                             (last_bs[:, 0:1], last_bs[:, 1:2], dst_last)):
                    nc.vector.tensor_reduce(least, targets, AX.X, ALU.min).then_inc(dve_step, 1)
                    nc.vector.tensor_reduce(most, targets, AX.X, ALU.max).then_inc(dve_step, 1)
                steps[0] += 6
                dve.wait_ge(dve_step, steps[0])
                step(nc.vector.tensor_tensor(span_g[:, :], span_g[:, :], base_g[:, :], ALU.subtract))
                step(nc.vector.tensor_tensor(span_d[:, :], span_d[:, :], base_d[:, :], ALU.subtract))
                nc.vector.tensor_tensor(last_bs[:, 1:2], last_bs[:, 1:2], last_bs[:, 0:1],
                                        ALU.subtract).then_inc(bases_found, 1)

            dve.wait_ge(w_product, 1)
            w_out = w_f32.rearrange("p (r o) -> p o r", o=F)
            w_in = psum[:, :].rearrange("p (o r) -> p o r", r=RELS)
            nc.vector.tensor_copy(w_out[:, F // 2:F, :], w_in[:, F // 2:F, :]).then_inc(w_copied, 1)
            dve.wait_ge(w_copied, 2)
            dve.sem_inc(dve_free, 2)

            def split_w(u):
                at = slice(u * UNIT, (u + 1) * UNIT)
                dve.wait_ge(w_high_ready, 2 * (u + 1))
                step(nc.vector.tensor_tensor(w_rem, w_f32[:, at], w_high[:, at], ALU.subtract))
                step(nc.vector.tensor_copy(w_mid[:, at], w_rem))
                nc.vector.tensor_tensor(w_lowhigh[0:F, at], w_rem[0:F, :], w_mid[0:F, at],
                                        ALU.subtract).then_inc(w_parts, 1)
                dve.wait_ge(w_parts, u + 1)

            def split_x(tile, t):
                wait(dve, unit_full, UNITS * (tile - 1))
                x_tile = bass.ds(tile * P, P)
                nc.vector.tensor_copy(x_hm[:, t, :], xT[:, x_tile]).then_inc(x_step, 1)
                nc.vector.tensor_copy(x_hl[:, t, :], xT[:, x_tile]).then_inc(x_step, 1)
                dve.wait_ge(x_step, 4 * tile + 2)
                nc.vector.tensor_tensor(x_rem[F:P, t, :], xT[F:P, x_tile], x_hl[F:P, t, :],
                                        ALU.subtract).then_inc(x_step, 1)
                dve.wait_ge(x_step, 4 * tile + 3)
                nc.vector.tensor_copy(x_hm[F:P, t, :], x_rem[F:P, t, :]).then_inc(x_step, 1)
                dve.wait_ge(x_step, 4 * tile + 4)
                nc.vector.tensor_tensor(x_hl[F:P, t, :], x_rem[F:P, t, :], x_hm[F:P, t, :],
                                        ALU.subtract).then_inc(x_parts, 1)

            split_w(0)
            dve.wait_ge(s_x, 16)
            split_x(0, 0)
            for u in range(1, UNITS):
                split_w(u)
            def table_turn(i, first=False, last=False):
                for t in range(2):
                    tile = 2 * i + t
                    if not (last and t == 1):
                        split_x(tile + 1, (t + 1) % 2)
                    for u in range(1, UNITS, 2):
                        dve.wait_ge(unit_full, UNITS * tile + u + 1)
                        if not first:
                            dve.wait_ge(stored[t * UNITS + u], 16 * i)
                        nc.vector.tensor_copy(stage(t, u), unit_psum(u)).then_inc(dve_free, 1)

            dve.wait_ge(s_x_rest, 16)
            table_turn(0, first=True)
            find_bases()
            with dve.Fori(1, KEY_TURN) as i:
                table_turn(i)
            dve.wait_ge(bases_loaded, 64)
            nc.vector.tensor_tensor(relative[:, :], dst_key[:, 0:DIRECT_TILES], direct_base_row[:, :],
                                    ALU.subtract).then_inc(keys_made, 1)
            dve.wait_ge(keys_made, 1)
            nc.vector.scalar_tensor_tensor(out=direct_key[:, :], in0=relative[:, :], scalar=float(RELS),
                                           in1=direct_key[:, :], op0=ALU.mult, op1=ALU.add).then_inc(keys_made, 1)
            whole = dst_key[:, 0:GROUPS * GROUP].rearrange("p (g k) -> p g k", k=GROUP)
            bases = base_row[:, :].unsqueeze(2).broadcast_to([P, GROUPS, GROUP])
            nc.vector.tensor_tensor(whole, whole, bases, ALU.subtract).then_inc(keys_made, 1)
            nc.vector.tensor_reduce(span_max[:, 0:1], span_row[:, :], AX.X, ALU.max).then_inc(keys_made, 1)
            nc.vector.tensor_reduce(span_max[:, 1:2], direct_span_row[:, :], AX.X, ALU.max).then_inc(keys_made, 1)
            dve.wait_ge(keys_made, 5)
            dve.sem_inc(flag_ready, 1)
            with dve.Fori(KEY_TURN, NODE_TILES // 2 - 1) as i:
                table_turn(i)
            table_turn(NODE_TILES // 2 - 1, last=True)
            table_stored(dve)

            def indices(g, q):
                slots = slice(q * GROUP, (q + 1) * GROUP)
                nc.vector.tensor_copy(index_slot[:, slots], row_index[:, bass.ds(g * GROUP, GROUP)]
                                      ).then_inc(index_ready, 1)

            dve.sem_inc(sum_free, QUADS)
            dve.wait_ge(constants, 9)
            dve.wait_ge(s_weight, 16)
            group_span, direct_span = modes(dve)

            def selection(g, s):
                for k in range(GROUP):
                    t = g * GROUP + k
                    last = nc.vector.tensor_scalar(select[:, s, k, :], node_iota[:, 0:WINDOW],
                                                   dst_key[:, bass.ds(t, 1)], weight[:, bass.ds(t, 1)],
                                                   ALU.is_equal, ALU.mult)
                last.then_inc(select_ready, 1)

            def load_bases(row, first, count):
                return nc.values_load_multi_w_load_instructions(
                    row[0:1, bass.ds(first, count)], engines=[mybir.EngineType.DVE], min_val=0, max_val=N_NODES - 1,
                    skip_runtime_bounds_check_because="targets are node numbers")[1]

            def add_window(n, q, base):
                window = hT[:, bass.ds(base, WINDOW)]
                dve.wait_ge(sum_free, n + QUADS)
                nc.vector.tensor_tensor(window, window, psum[0:F, q * BANK:q * BANK + WINDOW],
                                        ALU.add).then_inc(sum_free, 1)

            def prepare_pair(n, i, q):
                t = n * PAIR
                dve.wait_ge(direct_loaded[q], 16 * (i + 1))
                nc.vector.tensor_tensor(scaled[:, q % 2, :].rearrange("p (j f) -> p j f", j=PAIR),
                                        direct_x[:, q, :].rearrange("p (j f) -> p j f", j=PAIR),
                                        weight[:, bass.ds(t, PAIR)].unsqueeze(2).broadcast_to([P, PAIR, F]),
                                        ALU.mult).then_inc(pair_scaled, 1)
                wait(dve, pairs_summed, n - 1)

            def select_pair(n, q, j):
                last = nc.vector.tensor_scalar(pair_select[:, q % 2, j, :], key_iota[:, :],
                                               direct_key[:, bass.ds(n * PAIR + j, 1)], None, ALU.is_equal)
                if j == PAIR - 1:
                    last.then_inc(pair_selected, 1)

            def remainder(n, q):
                dve.wait_ge(pair_high, n + 1)
                nc.vector.tensor_tensor(scaled_rem[:, q % 2, :], scaled[:, q % 2, :], parts[:, 0, q % 2, :],
                                        ALU.subtract).then_inc(pair_rem, 1)

            def finish_pair(n, q):
                dve.wait_ge(pair_mid, n + 1)
                nc.vector.tensor_tensor(parts[:, 2, q % 2, :], scaled_rem[:, q % 2, :], parts[:, 1, q % 2, :],
                                        ALU.subtract).then_inc(pair_low, 1)

            def add_direct(i, j, base):
                if j == 0:
                    dve.wait_ge(transformed, i + 1)
                else:
                    dve.wait_ge(tile_added, i * DIRECT_PER_TURN + j)
                window = hT[:, bass.ds(base, NARROW)]
                at = 6 * BANK + j * NARROW
                nc.vector.tensor_tensor(window, window, psum[0:F, at:at + NARROW], ALU.add).then_inc(tile_added, 1)
                if j == DIRECT_PER_TURN - 1:
                    dve.wait_ge(tile_added, (i + 1) * DIRECT_PER_TURN)
                    dve.sem_inc(turns_added, 1)

            def narrow_tail(first, turns):
                for n in range(turns * QUADS, GROUPS - first):
                    g = first + n
                    if g + 1 < GROUPS:
                        selection(g + 1, (n + 1) % 2)
                    dve.wait_ge(window_summed, n + 1)
                    add_window(n, n % QUADS, load_bases(base_row, g, 1)[0])
                dve.wait_ge(sum_free, GROUPS - first + QUADS)

            with dve.If((group_span < WINDOW) & (direct_span < NARROW)):
                for q in range(QUADS):
                    indices(FIRST_GROUP + q, q)
                dve.wait_ge(h_zeroed, 3)
                dve.sem_inc(turns_added, 1)
                selection(FIRST_GROUP, 0)

                def both(i):
                    first = isinstance(i, int) and i == 0
                    for q in range(QUADS):
                        n = QUADS * i + q
                        g = FIRST_GROUP + n
                        adds = q >= 2 and not first

                        def add(k):
                            if adds:
                                j = (q - 2) * 4 + k
                                add_direct(i - 1, j, direct_bases[j])

                        prepare_pair(n, i, q)
                        if adds:
                            dve.wait_ge(sum_free, n + QUADS)
                        add(0)
                        select_pair(n, q, 0)
                        add(1)
                        select_pair(n, q, 1)
                        add(2)
                        remainder(n, q)
                        selection(g + 1, (q + 1) % 2)
                        if q == 0:
                            starts = load_bases(base_row, FIRST_GROUP + QUADS * i, QUADS)
                        if q == 1 and not first:
                            direct_bases = load_bases(direct_base_row, (i - 1) * DIRECT_PER_TURN, DIRECT_PER_TURN)
                        add(3)
                        finish_pair(n, q)
                        dve.wait_ge(window_summed, n + 1)
                        indices(g + QUADS, q)
                        if adds:
                            dve.wait_ge(tile_added, (i - 1) * DIRECT_PER_TURN + (q - 1) * 4)
                        add_window(n, q, starts[q])

                both(0)
                with dve.Fori(1, TURNS) as i:
                    both(i)
                narrow_tail(FIRST_GROUP, TURNS)
                last_bases = load_bases(direct_base_row, (TURNS - 1) * DIRECT_PER_TURN, DIRECT_PER_TURN)
                dve.wait_ge(sum_free, GROUPS - FIRST_GROUP + QUADS)
                for j in range(DIRECT_PER_TURN):
                    add_direct(TURNS - 1, j, last_bases[j])
            with dve.Else():
                for q in range(QUADS):
                    indices(q, q)
                dve.wait_ge(h_zeroed, 3)
                with dve.If(group_span < WINDOW):
                    selection(0, 0)
                    with dve.Fori(0, ALL_TURNS) as i:
                        starts = load_bases(base_row, QUADS * i, QUADS)
                        for q in range(QUADS):
                            g = QUADS * i + q
                            selection(g + 1, (q + 1) % 2)
                            dve.wait_ge(window_summed, g + 1)
                            indices(g + QUADS, q)
                            add_window(g, q, starts[q])
                    narrow_tail(0, ALL_TURNS)
                with dve.Else():
                    nc.vector.tensor_tensor(whole, whole, bases, ALU.add).then_inc(key_unshifted, 1)
                    dve.wait_ge(key_unshifted, 1)

                    def add_wide(g, q, w):
                        n = g * WIDE_WINDOWS + w
                        for k in range(GROUP):
                            t = g * GROUP + k
                            last = nc.vector.tensor_scalar(wide_select[:, k, :], wide_iota[:, :],
                                                           dst_key[:, bass.ds(t, 1)], weight[:, bass.ds(t, 1)],
                                                           ALU.is_equal, ALU.mult)
                        last.then_inc(select_ready, 1)
                        dve.wait_ge(window_summed, n + 1)
                        window = hT[:, bass.ds(w * WIDE, WIDE)]
                        nc.vector.tensor_tensor(window, window, psum[0:F, q * BANK:(q + 1) * BANK],
                                                ALU.add).then_inc(sum_free, 1)
                        dve.wait_ge(sum_free, n + 1 + QUADS)
                        nc.vector.tensor_scalar(wide_iota[:, :], wide_iota[:, :], float(WIDE), None,
                                                ALU.add).then_inc(iota_step, 1)
                        dve.wait_ge(iota_step, n + g + 2)

                    def group(g, q):
                        nc.vector.tensor_copy(wide_iota[:, :], node_iota[:, :]).then_inc(iota_step, 1)
                        dve.wait_ge(iota_step, g * (WIDE_WINDOWS + 1) + 1)
                        dve.sem_inc(wait_carrier, 1)
                        with dve.Fori(0, WIDE_WINDOWS) as w:
                            add_wide(g, q, w)

                    with dve.Fori(0, ALL_TURNS) as i:
                        for q in range(QUADS):
                            group(QUADS * i + q, q)
                            indices(QUADS * i + q + QUADS, q)
                    for g in range(ALL_TURNS * QUADS, GROUPS):
                        group(g, g % QUADS)
                dve.sem_inc(wait_carrier, 1)
            dve.sem_inc(h_done, 1)

            def add_y(c):
                c0, m = CHUNKS[c]
                dve.wait_ge(relu_ready, c + 1)
                nc.vector.tensor_tensor(xT[0:F, c0:c0 + m], hT[:, c0:c0 + m], xT[0:F, c0:c0 + m],
                                        ALU.add).then_inc(y_ready_dve, 1)

            for c, (c0, m) in enumerate(CHUNKS):
                if c == 0:
                    dve.wait_ge(res_free, RES_CHUNKS + 1)
                    add_y(0)
                if c % 3 == 1 and c + 2 < len(CHUNKS):
                    add_y(c + 2)
                if c % 3 == 0:
                    dve.wait_ge(y_ready_dve, c // 3 + 1)
                else:
                    dve.wait_ge(y_ready_pool, c - c // 3)
                nc.vector.bn_stats(stats[:, c, :], xT[0:F, c0:c0 + m]).then_inc(stats_ready, 1)
            dve.wait_ge(stats_ready, len(CHUNKS))
            nc.vector.bn_aggr(mv[:, :], stats[:, :, :].rearrange("f c s -> f (c s)")).then_inc(bn_step, 1)
            dve.wait_ge(bn_step, 2)
            nc.vector.reciprocal(affine[:, 1:2], affine[:, 0:1]).then_inc(bn_step, 1)
            dve.wait_ge(bn_step, 3)
            nc.vector.tensor_tensor(affine[:, 2:3], affine[:, 1:2], cols[:, 2:3], ALU.mult).then_inc(bn_step, 1)
            dve.wait_ge(bn_step, 4)
            nc.vector.tensor_tensor(affine[:, 3:4], mv[:, 0:1], affine[:, 2:3], ALU.mult).then_inc(bn_step, 1)
            nc.vector.tensor_scalar(affine[:, 5:6], affine[:, 2:3], 1.0 / F, None, ALU.mult).then_inc(bn_step, 1)
            dve.wait_ge(bn_step, 6)
            nc.vector.tensor_tensor(affine[:, 4:5], cols[:, 3:4], affine[:, 3:4], ALU.subtract).then_inc(bn_step, 1)
            dve.wait_ge(bn_step, 7)
            nc.vector.tensor_scalar(shift_diag[:, :], identity[:, :], affine[:, 4:5], None,
                                    ALU.mult).then_inc(bn_step, 1)
            nc.vector.tensor_scalar(combine[0:F, :], identity[:, :], affine[:, 2:3], affine[:, 5:6],
                                    ALU.mult, ALU.subtract).then_inc(bn_step, 1)
            nc.vector.tensor_scalar(combine[F:P, :], combine[F:P, :], 1.0 / F, None,
                                    ALU.subtract).then_inc(bn_step, 1)
            dve.wait_ge(shift_product, 1)
            nc.vector.tensor_reduce(shift_mean[:, :], psum[:, 0:F], AX.X, ALU.add).then_inc(shift_step, 1)
            dve.wait_ge(shift_step, 1)
            nc.vector.tensor_scalar(shift_mean[:, :], shift_mean[:, :], 1.0 / F, None, ALU.mult).then_inc(shift_step, 1)
            dve.wait_ge(shift_step, 2)
            nc.vector.tensor_scalar(shift_row[:, :], psum[:, 0:F], shift_mean[:, 0:1], None,
                                    ALU.subtract).then_inc(shift_step, 1)
            dve.wait_ge(shift_step, 3)
            for b in range(len(BLOCKS) + 2):
                if b < len(BLOCKS):
                    _, m, k = BLOCKS[b]
                    at = (4 + 2 * (b % 2)) * BANK
                    dve.wait_ge(z_product, b + 1)
                    if b >= ZS:
                        dve.wait_ge(z_stored[b % ZS], 16 * (b // ZS))
                    nc.vector.tensor_tensor(z_buf[0:m, b % ZS, 0:k * F].rearrange("p (k f) -> p k f", k=k),
                                            psum[0:m, at:at + 2 * k * F].rearrange("p (k f) -> p k f", k=k)[:, :, 0:F],
                                            shift_row[0:m, :].unsqueeze(1).broadcast_to([m, k, F]),
                                            ALU.add).then_inc(z_shifted, 1)
                if 1 <= b <= len(BLOCKS):
                    _, m, k = BLOCKS[b - 1]
                    dve.wait_ge(z_squared, b)
                    nc.vector.tensor_reduce(deviation[0:m, (b - 1) % ZS, 0, 0:k],
                                            squares[0:m, (b - 1) % 2, 0:k * F].rearrange("p (k f) -> p k f", k=k),
                                            AX.X, ALU.add).then_inc(var_ready, 1)
                if b >= 2:
                    _, m, k = BLOCKS[b - 2]
                    s = (b - 2) % ZS
                    dve.wait_ge(std_ready, b - 1)
                    nc.vector.reciprocal(deviation[0:m, s, 1, 0:k], deviation[0:m, s, 0, 0:k]).then_inc(inverse_ready, 1)
                    if b % 2 == 0:
                        dve.wait_ge(inverse_ready, b - 1)
                        z = z_buf[0:m, s, 0:k * F].rearrange("p (k f) -> p k f", k=k)
                        nc.vector.tensor_tensor(z, z, deviation[0:m, s, 1, 0:k].unsqueeze(2).broadcast_to([m, k, F]),
                                                ALU.mult).then_inc(z_ready_even, 1)


def kernel(x, src, dst, edge_type_64, edge_weight1, L0_gnn_basis, L0_gnn_comp, L0_gnn_bias, L0_gnn_res_w,
           L0_gnn_res_b, L0_gnn_gamma, L0_gnn_beta):
    import numpy as np
    import concourse.bacc as bacc
    from concourse.bass_utils import run_bass_kernel_spmd

    def tile_columns(a):
        a = np.asarray(a).reshape(-1)
        padded = np.zeros(TILE_COLUMNS * P, a.dtype)
        padded[:N_EDGES] = a
        return np.ascontiguousarray(padded.reshape(TILE_COLUMNS, P).T)

    def column(a):
        return np.ascontiguousarray(np.asarray(a).reshape(F, 1))

    xT = np.zeros((F, NODES_PADDED), np.float32)
    xT[:, :N_NODES] = np.asarray(x).T
    basis = np.asarray(L0_gnn_basis).transpose(0, 2, 1)
    basis = basis.reshape(BASES, F // 2, 2, F).transpose(2, 0, 1, 3).reshape(P, F // 2, F)
    basis2 = np.ascontiguousarray(np.concatenate([basis, basis], axis=2))
    arrays = {
        "x_rows": np.ascontiguousarray(np.asarray(x)),
        "x2T": np.concatenate([xT, xT], axis=0),
        "src_cols": tile_columns(src),
        "type_cols": tile_columns(edge_type_64),
        "dst_cols": tile_columns(dst),
        "dst_flat": np.ascontiguousarray(np.asarray(dst)),
        "weight_cols": tile_columns(edge_weight1),
        "basis2": basis2,
        "compT": np.ascontiguousarray(np.asarray(L0_gnn_comp).T),
        "bias_col": column(L0_gnn_bias),
        "res_wT": np.ascontiguousarray(np.asarray(L0_gnn_res_w).T),
        "res_b_col": column(L0_gnn_res_b),
        "gamma_col": column(L0_gnn_gamma),
        "beta_col": column(L0_gnn_beta),
    }
    nc = bacc.Bacc("TRN2", target_bir_lowering=False, num_devices=1)
    args = {name: nc.dram_tensor(name, a.shape, mybir.dt.from_np(a.dtype), kind="ExternalInput").ap()
            for name, a in arrays.items()}
    out = nc.dram_tensor("out", (N_NODES, F), mybir.dt.float32, kind="ExternalOutput").ap()
    gnn_program(nc, out=out, **args)
    result = run_bass_kernel_spmd(nc, [arrays], core_ids=[0])
    return result.results[0]["out"]
```
